# Optimizing a Trainium2 kernel written in Bass

```python
import numpy as np
import jax
import jax.numpy as jnp

def _softmax(x, axis=-1):
    return jax.nn.softmax(x, axis=axis)

def _gelu(x):
    return jax.nn.gelu(x, approximate=True)

def _silu(x):
    return jax.nn.silu(x)

def _sigmoid(x):
    return jax.nn.sigmoid(x)

def _layernorm(x, axis=-1, eps=1e-05):
    m = jnp.mean(x, axis=axis, keepdims=True)
    v = jnp.var(x, axis=axis, keepdims=True)
    return (x - m) / jnp.sqrt(v + eps)

def _scatter_add(tgt, idx, src, axis=0):
    return tgt.at[idx].add(src)

def _segment_sum(src, seg, n):
    return jax.ops.segment_sum(src, seg, n)
kernel_name = 'mk_conv_seq_d1_conv_nhwc512_r4_debddf'

def setup_inputs(seed: int=0):
    np.random.seed(seed)
    _w = jnp.asarray

    def _rec_inputs():
        import jax
        import jax.numpy as jnp
        _gk = jax.random.key(seed)
        x = -8.268e-05 + 0.9999 * jax.random.normal(jax.random.fold_in(_gk, 1), (32, 56, 56, 128), jnp.float32)
        return x
    x = _rec_inputs()

    def _L0_conv_setup():
        import jax, jax.numpy as jnp
        import numpy as np
        B, H, W, C = (32, 56, 56, 128)
        HEADS, WS, SS = (16, 7, 3)
        N = WS * WS
        HD = C // HEADS
        HID = 4 * C
        nWh, nWw = (H // WS, W // WS)
        nW = nWh * nWw

        def _rel_pos_index():
            coords = np.stack(np.meshgrid(np.arange(WS), np.arange(WS), indexing='ij'))
            cf = coords.reshape(2, -1)
            rel = (cf[:, :, None] - cf[:, None, :]).transpose(1, 2, 0).copy()
            rel[:, :, 0] += WS - 1
            rel[:, :, 1] += WS - 1
            rel[:, :, 0] *= 2 * WS - 1
            return rel.sum(-1)

        def _attn_mask():
            img = np.zeros((H, W))
            cnt = 0
            for h0, h1 in ((0, H - WS), (H - WS, H - SS), (H - SS, H)):
                for w0, w1 in ((0, W - WS), (W - WS, W - SS), (W - SS, W)):
                    img[h0:h1, w0:w1] = cnt
                    cnt += 1
            mw = img.reshape(nWh, WS, nWw, WS).transpose(0, 2, 1, 3).reshape(-1, N)
            diff = mw[:, None, :] - mw[:, :, None]
            return np.where(diff != 0, -100.0, 0.0).astype(np.float32)
        _REL_IDX = _rel_pos_index()
        _MASK = _attn_mask()

        def _ln(x, g, b, eps=1e-05):
            mu = x.mean(-1, keepdims=True)
            var = ((x - mu) ** 2).mean(-1, keepdims=True)
            return (x - mu) * jax.lax.rsqrt(var + eps) * g + b
        key = jax.random.key(seed)
        ks = jax.random.split(key, 8)
        s = lambda k, shape: jax.random.normal(k, shape, jnp.float32) * 0.02
        return {'x': jax.random.normal(ks[0], (B, H, W, C), jnp.float32), 'norm1_g': jnp.ones((C,), jnp.float32), 'norm1_b': jnp.zeros((C,), jnp.float32), 'qkv_w': s(ks[1], (3 * C, C)), 'qkv_b': jnp.zeros((3 * C,), jnp.float32), 'rel_pos_table': s(ks[2], ((2 * WS - 1) ** 2, HEADS)), 'proj_w': s(ks[3], (C, C)), 'proj_b': jnp.zeros((C,), jnp.float32), 'norm2_g': jnp.ones((C,), jnp.float32), 'norm2_b': jnp.zeros((C,), jnp.float32), 'fc1_w': s(ks[4], (HID, C)), 'fc1_b': jnp.zeros((HID,), jnp.float32), 'fc2_w': s(ks[5], (C, HID)), 'fc2_b': jnp.zeros((C,), jnp.float32)}
    _L0_conv_all = _L0_conv_setup()
    _L0_conv_in = {k: v for k, v in _L0_conv_all.items() if k in ('norm1_g', 'norm1_b', 'qkv_w', 'qkv_b', 'rel_pos_table', 'proj_w', 'proj_b', 'norm2_g', 'norm2_b', 'fc1_w', 'fc1_b', 'fc2_w', 'fc2_b')}
    del _L0_conv_all
    return {'x': x, 'L0_conv_norm1_g': _L0_conv_in['norm1_g'], 'L0_conv_norm1_b': _L0_conv_in['norm1_b'], 'L0_conv_qkv_w': _L0_conv_in['qkv_w'], 'L0_conv_qkv_b': _L0_conv_in['qkv_b'], 'L0_conv_rel_pos_table': _L0_conv_in['rel_pos_table'], 'L0_conv_proj_w': _L0_conv_in['proj_w'], 'L0_conv_proj_b': _L0_conv_in['proj_b'], 'L0_conv_norm2_g': _L0_conv_in['norm2_g'], 'L0_conv_norm2_b': _L0_conv_in['norm2_b'], 'L0_conv_fc1_w': _L0_conv_in['fc1_w'], 'L0_conv_fc1_b': _L0_conv_in['fc1_b'], 'L0_conv_fc2_w': _L0_conv_in['fc2_w'], 'L0_conv_fc2_b': _L0_conv_in['fc2_b']}

def reference(x, L0_conv_norm1_g, L0_conv_norm1_b, L0_conv_qkv_w, L0_conv_qkv_b, L0_conv_rel_pos_table, L0_conv_proj_w, L0_conv_proj_b, L0_conv_norm2_g, L0_conv_norm2_b, L0_conv_fc1_w, L0_conv_fc1_b, L0_conv_fc2_w, L0_conv_fc2_b):
    import jax
    import jax.numpy as jnp

    def _L0_conv_ref(x, norm1_g, norm1_b, qkv_w, qkv_b, rel_pos_table, proj_w, proj_b, norm2_g, norm2_b, fc1_w, fc1_b, fc2_w, fc2_b):
        import jax, jax.numpy as jnp
        import numpy as np
        B, H, W, C = (32, 56, 56, 128)
        HEADS, WS, SS = (16, 7, 3)
        N = WS * WS
        HD = C // HEADS
        HID = 4 * C
        nWh, nWw = (H // WS, W // WS)
        nW = nWh * nWw

        def _rel_pos_index():
            coords = np.stack(np.meshgrid(np.arange(WS), np.arange(WS), indexing='ij'))
            cf = coords.reshape(2, -1)
            rel = (cf[:, :, None] - cf[:, None, :]).transpose(1, 2, 0).copy()
            rel[:, :, 0] += WS - 1
            rel[:, :, 1] += WS - 1
            rel[:, :, 0] *= 2 * WS - 1
            return rel.sum(-1)

        def _attn_mask():
            img = np.zeros((H, W))
            cnt = 0
            for h0, h1 in ((0, H - WS), (H - WS, H - SS), (H - SS, H)):
                for w0, w1 in ((0, W - WS), (W - WS, W - SS), (W - SS, W)):
                    img[h0:h1, w0:w1] = cnt
                    cnt += 1
            mw = img.reshape(nWh, WS, nWw, WS).transpose(0, 2, 1, 3).reshape(-1, N)
            diff = mw[:, None, :] - mw[:, :, None]
            return np.where(diff != 0, -100.0, 0.0).astype(np.float32)
        _REL_IDX = _rel_pos_index()
        _MASK = _attn_mask()

        def _ln(x, g, b, eps=1e-05):
            mu = x.mean(-1, keepdims=True)
            var = ((x - mu) ** 2).mean(-1, keepdims=True)
            return (x - mu) * jax.lax.rsqrt(var + eps) * g + b
        shortcut = x
        y = _ln(x, norm1_g, norm1_b)
        y = jnp.roll(y, (-SS, -SS), axis=(1, 2))
        yw = y.reshape(B, nWh, WS, nWw, WS, C).transpose(0, 1, 3, 2, 4, 5).reshape(B * nW, N, C)
        qkv = yw @ qkv_w.T + qkv_b
        qkv = qkv.reshape(B * nW, N, 3, HEADS, HD).transpose(2, 0, 3, 1, 4)
        q, k, v = (qkv[0], qkv[1], qkv[2])
        scale = HD ** (-0.5)
        attn = jnp.einsum('bhqd,bhkd->bhqk', q * scale, k)
        bias = rel_pos_table[jnp.asarray(_REL_IDX.reshape(-1))].reshape(N, N, HEADS)
        attn = attn + bias.transpose(2, 0, 1)[None]
        attn = attn.reshape(B, nW, HEADS, N, N) + jnp.asarray(_MASK)[None, :, None]
        attn = jax.nn.softmax(attn.reshape(B * nW, HEADS, N, N), axis=-1)
        o = jnp.einsum('bhqk,bhkd->bhqd', attn, v)
        o = o.transpose(0, 2, 1, 3).reshape(B * nW, N, C)
        o = o @ proj_w.T + proj_b
        o = o.reshape(B, nWh, nWw, WS, WS, C).transpose(0, 1, 3, 2, 4, 5).reshape(B, H, W, C)
        o = jnp.roll(o, (SS, SS), axis=(1, 2))
        x = shortcut + o
        h = _ln(x, norm2_g, norm2_b)
        h = jax.nn.gelu(h @ fc1_w.T + fc1_b, approximate=False)
        h = h @ fc2_w.T + fc2_b
        return x + h

    def _gn(v, G=32, eps=1e-05):
        B_, H_, W_, C_ = v.shape
        g = v.reshape(B_, H_, W_, G, C_ // G)
        m = jnp.mean(g, axis=(1, 2, 4), keepdims=True)
        s = jnp.var(g, axis=(1, 2, 4), keepdims=True)
        return ((g - m) / jnp.sqrt(s + eps)).reshape(v.shape)

    def _ln_c(v, eps=1e-06):
        m = jnp.mean(v, axis=-1, keepdims=True)
        s = jnp.var(v, axis=-1, keepdims=True)
        return (v - m) / jnp.sqrt(s + eps)

    def _ln_t(v, eps=1e-05):
        m = jnp.mean(v, axis=-1, keepdims=True)
        s = jnp.var(v, axis=-1, keepdims=True)
        return (v - m) / jnp.sqrt(s + eps)

    def _to_tokens(v):
        B_, H_, W_, C_ = v.shape
        return v.reshape(B_, H_ * W_, C_)

    def _from_tokens(t, like):
        return t.reshape(like.shape)
    x = _L0_conv_ref(x, L0_conv_norm1_g, L0_conv_norm1_b, L0_conv_qkv_w, L0_conv_qkv_b, L0_conv_rel_pos_table, L0_conv_proj_w, L0_conv_proj_b, L0_conv_norm2_g, L0_conv_norm2_b, L0_conv_fc1_w, L0_conv_fc1_b, L0_conv_fc2_w, L0_conv_fc2_b)
    return x

_drawn_inputs = setup_inputs


def setup_inputs(seed=0):
    import zlib

    import numpy as np

    out = dict(_drawn_inputs(seed))
    spreads = {'L0_conv_norm1_g': (1.0, 0.6),
     'L0_conv_norm1_b': (0.0, 0.8),
     'L0_conv_qkv_b': (0.0, 0.342),
     'L0_conv_proj_b': (0.0, 0.1),
     'L0_conv_norm2_g': (1.0, 0.6),
     'L0_conv_norm2_b': (0.0, 0.8),
     'L0_conv_fc1_b': (0.0, 0.331),
     'L0_conv_fc2_b': (0.0, 0.1)}
    factors = {'L0_conv_qkv_w': 5.525, 'L0_conv_rel_pos_table': 27.182}
    for name, (base, spread) in spreads.items():
        noise = np.random.default_rng([zlib.crc32(name.encode()), seed]).standard_normal(out[name].shape)
        drawn = base * np.exp(spread * noise) if base else spread * noise
        out[name] = jnp.asarray(drawn.astype(out[name].dtype))
    for name, factor in factors.items():
        out[name] = (out[name] * factor).astype(out[name].dtype)
    return out
```

```python
from contextlib import ExitStack

import numpy as np
import concourse.bass as bass
from concourse import mybir

F32 = mybir.dt.float32
F16 = mybir.dt.float16
ALU = mybir.AluOpType
ACT = mybir.ActivationFunctionType
AX_X = mybir.AxisListType.X

B, H, W, C = 32, 56, 56, 128
WS, SS = 7, 3
NH = 16
HD = C // NH
HID = 4 * C
CH = HID // C
NW = W // WS
WT = WS * WS
BT = NW * WT
TP = 2 * W
PAIR = 2 * WT
PAIRS_OF_IMAGES = B // 2
BANDS = H // WS
STEPS = BANDS * PAIRS_OF_IMAGES
EDGE = (BANDS - 1) * PAIRS_OF_IMAGES
HB = NH // 2
VC = HD + 1
NG, NR = 4, 4
EPS = 1e-5
HALVES = ((0, 4), (4, 7))
NH2 = NH // 2
GR = 2 * HD
ST_ROWS = 6 * GR + 4
MX_ROWS = WT + 2 * GR
LOOP_1 = (3, EDGE - 3)
LOOP_2 = (EDGE + 3, STEPS - 3)


def swin_block_kernel(nc, x, wqT, wkT, wvT, wpT, w1T, w2T, cols, rows, tableT, ident, eye2,
                      wmask, part, masks, ones4, out):
    xr = x.rearrange("b h w c -> (b h) w c")
    outr = out.rearrange("b h w c -> (b h) w c")
    ctx = ExitStack()

    def sb(name, shape, dt=F32):
        return ctx.enter_context(nc.sbuf_tensor(name, shape, dt))

    def sem(name):
        return ctx.enter_context(nc.semaphore(name))

    with ctx:
        w_q, w_k, w_v, w_p = (sb(n, [C, C]) for n in ("w_q", "w_k", "w_v", "w_p"))
        w_1 = sb("w_1", [C, HID])
        w_2 = sb("w_2", [C, CH, C])
        col = sb("col", [C, 7 + CH])
        G1, B1, G2, B2, BQ, BK, BV, BF = range(8)
        proj_b = sb("proj_b", [TP, C])
        fc2_b = sb("fc2_b", [TP, C])
        bv_wide = sb("bv_wide", [C, TP])
        idn = sb("idn", [C, C])
        idn16 = sb("idn16", [WT, WT], F16)
        eye_pair = sb("eye_pair", [PAIR, PAIR], F16)
        own = sb("own", [PAIR, 2])
        is_part = sb("is_part", [PAIR, 2])
        mask = sb("mask", [PAIR, 4, WT])
        bias_t = sb("bias_t", [PAIR, 4, NH * WT], F16)
        half = sb("half", [TP, WS])
        x_in = sb("x_in", [TP, WS, C])
        st1, st2 = sb("st1", [TP, WS, 6]), sb("st2", [TP, WS, 6])
        mv1, mv2 = sb("mv1", [TP, WS, 2]), sb("mv2", [TP, WS, 2])
        ve1, ve2 = sb("ve1", [TP, WS]), sb("ve2", [TP, WS])
        rs1, rs2 = sb("rs1", [TP, WS]), sb("rs2", [TP, WS])
        mr1, mr2 = sb("mr1", [TP, WS]), sb("mr2", [TP, WS])
        nm1, nm2 = sb("nm1", [TP, WS]), sb("nm2", [TP, WS])
        z1, z2 = sb("z1", [TP, WS, C]), sb("z2", [TP, WS, C])
        yT = sb("yT", [C, NW, 2, WT])
        q_hi_own, k_hi_own, k_lo_own = (sb(n, [C, 2, NW, 2, WT], F16)
                                        for n in ("q_hi_own", "k_hi_own", "k_lo_own"))
        q_hi_pad, q_lo_pad, k_hi_pad = (sb(n, [C, 2, 2, BT], F16) for n in ("q_hi_pad", "q_lo_pad", "k_hi_pad"))
        mx_q = sb("mx_q", [MX_ROWS, NH2, NW * PAIR], F16)
        mx_k = [sb(f"mx_k{e}", [MX_ROWS, NH2, 2 * BT], F16) for e in range(2)]
        st_q = [sb(f"st_q{e}", [ST_ROWS, NH2, 2 * BT], F16) for e in range(2)]
        st_k = [sb(f"st_k{e}", [ST_ROWS, NH2, NW * PAIR], F16) for e in range(2)]
        neg_max = sb("neg_max", [PAIR, NW, NH])
        neg_maxT = sb("neg_maxT", [NH, 2, NW, WT], F16)
        v_own = sb("v_own", [PAIR, NW, NH, 2 * VC])
        probs = sb("probs", [PAIR, 2, NH * WT])
        pv_sb = sb("pv_sb", [C, NG, BT])
        pv_sum = sb("pv_sum", [C, NG, BT])
        oT_raw = sb("oT_raw", [C, 2, BT])
        sums = sb("sums", [C, 2, BT])
        r_sums = sb("r_sums", [C, 2, BT])
        oT = sb("oT", [C, WS, TP])
        x_res = sb("x_res", [TP, WS, C])
        x1 = sb("x1", [TP, WS, C])
        x1_b = sb("x1_b", [TP, WS, C])
        hT = sb("hT", [C, WS * TP])
        hid = sb("hid", [C, CH, WS * TP])
        y_out = sb("y_out", [TP, WS, C])
        bias_f, bias_k = (hid[0:PAIR, j, :].rearrange("p (h q) -> p h q", h=NH) for j in range(2))
        bias_hi, bias_lo = (hid[0:PAIR, 2, :].bitcast(F16).rearrange("p (a h q) -> p a h q", a=2, h=NH)[:, a]
                            for a in range(2))
        bias_r = hid[0:WT, 3, :].rearrange("p (h q) -> p h q", h=NH)
        bias_dram = nc.dram_tensor("bias_dram", [WS, NH, (2 * WS - 1) * WS], F32, kind="Internal").ap()

        ps = ctx.enter_context(nc.psum_tensor("ps", [C, 8, 512], F32))

        s_apart = {nc.gpsimd.engine: sem("waits_of_gpsimd"), nc.vector.engine: sem("waits_of_vector"),
                   nc.sync.engine: sem("waits_of_sync")}

        def tokens_of(bank):
            return ps[:, bank:bank + 2, :].rearrange("p b (i c) -> p (b i) c", c=C)

        (s_w, s_const, s_x, s_st1, s_ln1, s_ve1, s_rs1, s_mr1, s_nm1, s_z1, s_t1, s_yT, s_qk, s_hi, s_lo,
         s_v, s_vown_a, s_vown_d, s_mx_dma, s_rows, s_max, s_maxT, s_negT, s_st_dma, s_neg_dma,
         s_st, s_exp, s_pv, s_pv_sb, s_o_dma, s_rsum, s_oT, s_proj, s_xres_dma, s_xres, s_x1,
         s_st2, s_ln2, s_ve2, s_rs2, s_mr2, s_nm2, s_z2, s_x1b, s_t2, s_hT, s_fc1, s_gelu, s_fc2,
         s_fin, s_stored, s_bd1, s_bd2, s_init, s_initp, s_inita, s_bt, s_bt_mm, s_bp_mm, s_ones, s_shuf, s_own) = (
            sem(n) for n in (
                "weights_in", "constants_in", "x_loaded", "stats1_done", "moments1_done", "var_eps1_done",
                "rstd1_done", "mean_rstd1_done", "neg_mean1_done", "z1_ready", "z1_transposed", "yT_ready",
                "qk_projected", "qk_high_ready", "qk_low_ready", "v_projected", "v_own_by_scalar",
                "v_own_by_vector", "max_operands_in", "max_logits_ready", "max_taken", "max_transposed",
                "neg_maxT_ready", "core_operands_in", "neg_max_in", "logits_ready", "exp_done", "pv_done",
                "pv_copied", "o_spread", "r_sums_ready", "oT_ready", "projected", "x_res_loaded",
                "x_res_biased", "x1_ready", "stats2_done", "moments2_done", "var_eps2_done", "rstd2_done",
                "mean_rstd2_done", "neg_mean2_done", "z2_ready", "x1_biased", "z2_transposed", "hT_ready",
                "fc1_done", "gelu_done", "fc2_done", "y_ready", "y_stored", "bias_strips_out", "bias_in",
                "vector_set_up", "gpsimd_set_up", "scalar_set_up", "bias_step", "bias_transposed",
                "proj_bias_ready", "ones_in", "sums_repeated", "padded_ready"))

        def exists(n):
            return not isinstance(n, int) or 0 <= n < STEPS

        def loads(n, edge):
            return 64 * (n + 1) - 32 * EDGE if edge else 32 * (n + 1)

        def band_dmas(eng, dram, tile, n, edge, store, signal):
            for im in range(2):
                if edge:
                    base = (n - EDGE) * (2 * H) + im * H
                    pieces = ((base + H - WS + SS, 0, WS - SS), (base, WS - SS, SS))
                else:
                    base = (n % PAIRS_OF_IMAGES) * (2 * H) + (n // PAIRS_OF_IMAGES) * WS + SS + im * H
                    pieces = ((base, 0, WS),)
                for row, i0, k in pieces:
                    d = dram[bass.ds(row, k), :, :].rearrange("r w c -> w r c")
                    s = tile[W * im:W * im + W, i0:i0 + k, :]
                    eng.dma_start(d if store else s, s if store else d).then_inc(signal, 16)

        def apart(eng, sem_, value):
            eng.wait_ge(sem_, value)
            eng.sem_inc(s_apart[eng.engine], 1)

        def turns(eng, body):
            def plain(a, b):
                for t in range(a, b):
                    body(t, lambda n: n >= EDGE, lambda k: (t + k) % 2)
            def loop(a, b, edge):
                with eng.Fori(a, b - 1, 2) as t:
                    for later in range(2):
                        body(t + later, lambda n: edge, lambda k: (a + later + k) % 2)
            plain(-2, LOOP_1[0])
            loop(*LOOP_1, False)
            plain(LOOP_1[1], LOOP_2[0])
            loop(*LOOP_2, True)
            plain(LOOP_2[1], STEPS + 2)

        N_W, N_CONST = 9, 10
        block = ctx.enter_context(nc.Block())

        @block.sync
        def _(sp):
            for im, n in ((0, 0),):
                band_dmas(sp, xr, x_in, 0, False, False, s_x)
            for dst, src in ((w_q, wqT), (w_k, wkT), (w_v, wvT), (w_p, wpT), (w_1, w1T), (col, cols)):
                sp.dma_start(dst[:, :], src).then_inc(s_w, 16)
            sp.dma_start(w_2[:, :, :], w2T.rearrange("(a p) n -> p a n", p=C)).then_inc(s_w, 16)
            sp.dma_start(proj_b[:, :], rows[0:1, :].to_broadcast([TP, C])).then_inc(s_w, 16)
            sp.dma_start(fc2_b[:, :], rows[1:2, :].to_broadcast([TP, C])).then_inc(s_w, 16)
            strips = tableT.rearrange("h (a b) -> (h a) b", b=2 * WS - 1)
            for jk in range(WS):
                sp.dma_start(bias_dram[jk].rearrange("h (a b) -> (h a) b", b=WS),
                             strips[:, WS - 1 - jk:2 * WS - 1 - jk]).then_inc(s_bd1, 16)
            sp.wait_ge(s_bd1, 16 * WS)
            for copy in range(2):
                for ik in range(WS):
                    r = copy * WT + ik * WS
                    sp.dma_start(bias_f[r:r + WS, :, :],
                                 bias_dram[:, :, (WS - 1 - ik) * WS:(WS - 1 - ik) * WS + WT]).then_inc(s_bd2, 16)

            def body(t, edge, odd):
                n = t - 1
                if exists(n):
                    apart(sp, s_shuf, 2 * (n + 1))
                    if not isinstance(n, int) or n > 0:
                        sp.wait_ge(s_oT, n)
                    for src, dst in ((pv_sb, oT_raw), (pv_sum, sums)):
                        for r in range(NR):
                            for im in range(2):
                                p = 32 * r + VC * im
                                sp.dma_start(dst[32 * r:32 * r + 32, im, :],
                                             src[p:p + HD, :, :]).then_inc(s_o_dma, 16)
                    if not isinstance(n, int) or n > 0:
                        sp.wait_ge(s_x1, n)
                    band_dmas(sp, xr, x_res, n, edge(n), False, s_xres_dma)
                n = t + 1
                if exists(n):
                    if not isinstance(n, int) or n > 0:
                        apart(sp, s_rows, NW * n)
                    else:
                        sp.wait_ge(s_init, 2)
                    sp.wait_ge(s_lo, 4 * (n + 1))
                    for im in range(2):
                        rows_ = slice(WT + GR * im, WT + GR * (im + 1))
                        sp.dma_start(mx_k[edge(n)][rows_, :, :],
                                     k_hi_pad[:, im, :, :].rearrange("c e q -> c (e q)")).then_inc(s_mx_dma, 16)
                        sp.dma_start(mx_q[rows_, :, :],
                                     q_hi_own[:, im, :, :, :].rearrange("c w m q -> c (w m q)")
                                     ).then_inc(s_mx_dma, 16)
                    if not isinstance(n, int) or n > 1:
                        sp.wait_ge(s_st, NW * (n - 1))
                    for p, (qq, kk) in enumerate(((q_hi_pad, k_hi_own), (q_hi_pad, k_lo_own),
                                                  (q_lo_pad, k_hi_own))):
                        for im in range(2):
                            rows_ = slice(2 * GR * p + GR * im, 2 * GR * p + GR * (im + 1))
                            sp.dma_start(st_q[odd(1)][rows_, :, :],
                                         qq[:, im, :, :].rearrange("c e q -> c (e q)")).then_inc(s_st_dma, 16)
                            sp.dma_start(st_k[odd(1)][rows_, :, :],
                                         kk[:, im, :, :, :].rearrange("c w m q -> c (w m q)")
                                         ).then_inc(s_st_dma, 16)
                n = t + 3
                if exists(n):
                    sp.wait_ge(s_z1, n)
                    band_dmas(sp, xr, x_in, n, edge(n), False, s_x)
                n = t - 2
                if exists(n):
                    sp.wait_ge(s_fin, 2 * (n + 1))
                    band_dmas(sp, outr, y_out, n, edge(n), True, s_stored)
                n = t + 1
                if exists(n):
                    sp.wait_ge(s_negT, n + 1)
                    for im in range(2):
                        for e in range(2):
                            row = 6 * GR + 2 * im + e
                            sp.dma_start(st_q[odd(1)][row:row + 1, :, e * BT:(e + 1) * BT],
                                         neg_maxT[e:NH:2, im, :, :].rearrange("h w q -> h (w q)")
                                         ).then_inc(s_neg_dma, 16)

            turns(sp, body)
            sp.wait_ge(s_stored, loads(STEPS - 1, True))

        @block.gpsimd
        def _(pool):
            for dst, src in ((idn, ident), (eye_pair, eye2), (own, wmask), (is_part, part)):
                pool.dma_start(dst[:, :], src).then_inc(s_const, 16)
            pool.dma_start(mask[:, :, :], masks).then_inc(s_const, 16)
            nc.gpsimd.memset(half[:, :], -0.5)
            for tile in (q_hi_own, k_hi_own, k_lo_own):
                nc.gpsimd.memset(tile[:, :, :, :, :], 0.0)
            for tile in (q_hi_pad, q_lo_pad, k_hi_pad):
                last = nc.gpsimd.memset(tile[:, :, :, :], 0.0)
            for e in range(2):
                pool.dma_start(st_k[e][6 * GR:6 * GR + 4, :, :], ones4).then_inc(s_ones, 16)
            last.then_inc(s_initp, 1)

            def norm(n, s_mom, mv, ve, s_ve, rs, s_rs, mr, s_mr, nm, s_nm, src, z, s_free, s_z):
                apart(pool, s_mom, n + 1)
                nc.gpsimd.tensor_scalar(ve[:, :], mv[:, :, 1], 1.0, EPS, ALU.mult, ALU.add).then_inc(s_ve, 1)
                pool.wait_ge(s_ve, n + 1)
                nc.gpsimd.tensor_tensor(rs[:, :], ve[:, :], half[:, :], ALU.pow).then_inc(s_rs, 1)
                pool.wait_ge(s_rs, n + 1)
                nc.gpsimd.tensor_tensor(mr[:, :], mv[:, :, 0], rs[:, :], ALU.mult).then_inc(s_mr, 1)
                apart(pool, s_mr, n + 1)
                nc.gpsimd.tensor_scalar(nm[:, :], mr[:, :], -1.0, 0.0, ALU.mult, ALU.add).then_inc(s_nm, 1)
                pool.wait_ge(s_nm, n + 1)
                if not isinstance(n, int) or n > 0:
                    apart(pool, s_free, n)
                for i in range(WS):
                    last = nc.gpsimd.tensor_scalar(z[:, i, :], src[:, i, :], rs[:, i:i + 1], nm[:, i:i + 1],
                                                   ALU.mult, ALU.add)
                last.then_inc(s_z, 1)

            def body(t, edge, odd):
                n = t - 2
                if exists(n):
                    norm(n, s_ln2, mv2, ve2, s_ve2, rs2, s_rs2, mr2, s_mr2, nm2, s_nm2, x1, z2, s_t2, s_z2)
                    if not isinstance(n, int) or n > 0:
                        pool.wait_ge(s_fin, 2 * n)
                    nc.gpsimd.tensor_tensor(x1_b[:, :, :], x1[:, :, :],
                                            fc2_b[:, :].unsqueeze(1).to_broadcast([TP, WS, C]),
                                            ALU.add).then_inc(s_x1b, 1)
                n = t + 2
                if exists(n):
                    norm(n, s_ln1, mv1, ve1, s_ve1, rs1, s_rs1, mr1, s_mr1, nm1, s_nm1, x_in, z1, s_t1, s_z1)
                n = t - 1
                if exists(n):
                    if isinstance(n, int) and n == 0:
                        pool.wait_ge(s_w, 16 * N_W)
                        pool.wait_ge(s_init, 2)
                    pool.wait_ge(s_xres_dma, loads(n, edge(n)))
                    nc.gpsimd.tensor_tensor(x_res[:, :, :], x_res[:, :, :],
                                            proj_b[:, :].unsqueeze(1).to_broadcast([TP, WS, C]),
                                            ALU.add).then_inc(s_xres, 1)

            turns(pool, body)

        @block.scalar
        def _(act):
            act.wait_ge(s_w, 16 * N_W)
            nc.scalar.mul(w_q[:, :], w_q[:, :], HD ** -0.5).then_inc(s_inita, 1)
            nc.scalar.mul(col[:, BQ:BQ + 1], col[:, BQ:BQ + 1], HD ** -0.5).then_inc(s_inita, 1)
            act.wait_ge(s_inita, 2)

            def exp_pair(n, w):
                act.wait_ge(s_st, NW * n + w + 1)
                if w >= 2 or not isinstance(n, int) or n > 0:
                    act.wait_ge(s_pv, NW * n + w - 1)
                nc.scalar.activation(probs[:, w % 2, :].rearrange("p (b c) -> p b c", b=2),
                                     ps[0:PAIR, 2:4, 0:HB * WT], ACT.Exp).then_inc(s_exp, 1)

            def copy_pv(n, w):
                act.wait_ge(s_pv, NW * n + w + 1)
                if w == 0 and (not isinstance(n, int) or n > 0):
                    act.wait_ge(s_o_dma, 256 * n)
                nc.scalar.activation(pv_sb[:, :, w * WT:(w + 1) * WT],
                                     ps[:, 4 + w % 2, 0:NG * WT].rearrange("p (g q) -> p g q", g=NG),
                                     ACT.Copy).then_inc(s_pv_sb, 1)

            def body(t, edge, odd):
                n = t
                if exists(n):
                    act.wait_ge(s_v, 2 * n + 1)
                    if not isinstance(n, int) or n > 0:
                        act.wait_ge(s_pv, NW * n)
                    else:
                        act.wait_ge(s_init, 1)
                    for im in range(2):
                        last = nc.scalar.activation(
                            v_own[:, 0:4, :, VC * im:VC * im + HD],
                            ps[0:PAIR, 6, :].rearrange("p (w h d) -> p w h d", w=4, h=NH),
                            ACT.Copy, scale=own[:, im:im + 1])
                    last.then_inc(s_vown_a, 1)
                n = t + 1
                if exists(n):
                    act.wait_ge(s_t1, n + 1)
                    if not isinstance(n, int) or n > 0:
                        act.wait_ge(s_qk, 4 * n)
                        act.wait_ge(s_v, 2 * n)
                    src = tokens_of(0)[:, 0:WS, 0:TP].rearrange("p i (m c) -> p i m c", m=2)
                    dst = yT[:, :, :, :].rearrange("p w m (i j) -> p m w i j", i=WS)
                    last_w = NW - 1
                    kept = WS - SS
                    def put(o, a):
                        return nc.scalar.activation(o, a, ACT.Identity, scale=col[:, G1:G1 + 1],
                                                    bias=col[:, B1:B1 + 1])
                    for im in range(2):
                        put(dst[:, im, 0:last_w, :, :].rearrange("p w i j -> p i w j"),
                            src[:, :, im, SS:SS + last_w * WS].rearrange("p i (w j) -> p i w j", j=WS))
                    put(dst[:, :, last_w, :, 0:kept].rearrange("p m i j -> p i m j"),
                        src[:, :, :, W - kept:W])
                    put(dst[:, :, last_w, :, kept:WS].rearrange("p m i j -> p i m j"),
                        src[:, :, :, 0:SS]).then_inc(s_yT, 1)
                    if not isinstance(n, int) or n > 0:
                        act.wait_ge(s_mx_dma, 64 * n)
                        act.wait_ge(s_st_dma, 192 * n)
                    else:
                        act.wait_ge(s_initp, 1)
                    for j, (own_hi, bank, b) in enumerate(((q_hi_own, 6, BQ), (q_hi_own, 7, BQ),
                                                           (k_hi_own, 0, BK), (k_hi_own, 1, BK))):
                        im = j % 2
                        act.wait_ge(s_qk, 4 * n + j + 1)
                        nc.scalar.activation(own_hi[:, im, :, im, :],
                                             ps[:, bank, 0:BT].rearrange("p (w q) -> p w q", w=NW), ACT.Identity,
                                             bias=col[:, b:b + 1]).then_inc(s_hi, 1)
                n = t
                if exists(n):
                    for w in range(4):
                        exp_pair(n, w)
                        if w > 0:
                            copy_pv(n, w - 1)
                    copy_pv(n, 3)
                n = t - 2
                if exists(n):
                    if not isinstance(n, int) or n > 0:
                        act.wait_ge(s_fc2, 2 * n)
                    for m in range(2 * CH):
                        c, (i0, i1) = m % CH, HALVES[m // CH]
                        act.wait_ge(s_fc1, 2 * CH * n + m + 1)
                        nc.scalar.activation(hid[:, c, i0 * TP:i1 * TP], ps[:, 2 + m % 4, 0:(i1 - i0) * TP],
                                             ACT.Gelu, bias=col[:, BF + c:BF + c + 1]).then_inc(s_gelu, 1)
                n = t
                if exists(n):
                    for w in range(4, NW):
                        exp_pair(n, w)
                        if w > 4:
                            copy_pv(n, w - 1)
                    copy_pv(n, NW - 1)
            turns(act, body)

        @block.vector
        def _(dve):
            steps = [0]
            sum_rows = [HD + VC * (p // VC) if p < 2 * VC else HD for p in range(32)]

            def then(ins):
                steps[0] += 1
                ins.then_inc(s_bt, 1)
                dve.wait_ge(s_bt, steps[0])

            def moments(n, src, st, s_st_, mv, s_mv):
                for i in range(WS):
                    last = nc.vector.bn_stats(st[:, i, :], src[:, i, :])
                last.then_inc(s_st_, 1)
                apart(dve, s_st_, n + 1)
                for i in range(WS):
                    last = nc.vector.bn_aggr(mv[:, i, :], st[:, i, :])
                last.then_inc(s_mv, 1)

            def repeat_sums(n, p):
                dve.wait_ge(s_pv_sb, NW * n + 4 * (p + 1))
                if not isinstance(n, int) or n > 0:
                    apart(dve, s_o_dma, 256 * n)
                ws = slice(4 * p * WT, 4 * (p + 1) * WT)
                nc.vector.stream_shuffle(pv_sum[:, :, ws], pv_sb[:, :, ws], sum_rows).then_inc(s_shuf, 1)

            def norm1(n, edge):
                dve.wait_ge(s_x, loads(n, edge(n)))
                if not isinstance(n, int) or n > 0:
                    dve.wait_ge(s_z1, n)
                moments(n, x_in, st1, s_st1, mv1, s_ln1)

            norm1(0, lambda n: False)
            nc.vector.memset(ps[:, 4:6, 0:NG * WT], 0.0)
            nc.vector.memset(bv_wide[:, :], 0.0)
            for e in range(2):
                nc.vector.memset(st_q[e][6 * GR:6 * GR + 4, :, :], 0.0)
            then(nc.vector.memset(v_own[:, :, :, :], 0.0))
            dve.wait_ge(s_const, 16 * 5)
            dve.wait_ge(s_w, 16 * N_W)
            then(nc.vector.tensor_copy(idn16[:, :], idn[0:WT, 0:WT]))
            nc.vector.tensor_copy(mx_q[0:WT, :, :].rearrange("p g (w q) -> p (g w) q", q=WT),
                                  idn16[:, :].unsqueeze(1).to_broadcast([WT, NH2 * NW * 2, WT]))
            for im in range(2):
                nc.vector.tensor_copy(v_own[:, :, :, VC * im + HD].rearrange("p w h -> p (w h)"),
                                      own[:, im:im + 1].to_broadcast([PAIR, NW * NH]))
            then(nc.vector.tensor_scalar(bv_wide[:, :], bv_wide[:, :], col[:, BV:BV + 1], None, ALU.add))
            dve.wait_ge(s_bp_mm, 1)
            then(nc.vector.tensor_tensor(proj_b[:, :], proj_b[:, :], ps[0:TP, 7, 0:C], ALU.add))
            dve.wait_ge(s_bd2, 16 * 2 * WS)
            for kind in range(4):
                then(nc.vector.tensor_tensor(bias_k[:, :, :], bias_f[:, :, :],
                                             mask[:, kind, :].unsqueeze(1).to_broadcast([PAIR, NH, WT]), ALU.add))
                then(nc.vector.tensor_copy(bias_hi[:, :, :], bias_k[:, :, :]))
                then(nc.vector.tensor_tensor(bias_lo[:, :, :], bias_k[:, :, :], bias_hi[:, :, :], ALU.subtract))
                then(nc.vector.tensor_scalar(bias_lo[:, :, :], bias_lo[:, :, :], is_part[:, 1:2], None, ALU.mult))
                then(nc.vector.scalar_tensor_tensor(bias_t[:, kind, :], bias_hi[:, :, :].rearrange("p h q -> p (h q)"),
                                                    is_part[:, 0:1],
                                                    bias_lo[:, :, :].rearrange("p h q -> p (h q)"),
                                                    ALU.mult, ALU.add))
            dve.wait_ge(s_bt_mm, 1)
            for b in range(2):
                then(nc.vector.tensor_copy(bias_r[:, HB * b:HB * (b + 1), :],
                                           ps[0:WT, b, 0:HB * WT].rearrange("p (h k) -> p h k", h=HB)))
            for kind in range(4):
                first = kind % 2 == 0
                for w in (range(NW - 1) if first else (NW - 1,)):
                    last = nc.vector.tensor_tensor(
                        mx_k[kind // 2][0:WT, :, :].rearrange("p g (e w k) -> p (g e) w k", e=2, w=NW)[:, :, w, :],
                        bias_r[:, :, :],
                        mask[0:WT, kind, :].unsqueeze(1).to_broadcast([WT, NH, WT]), ALU.add)
            then(last)
            nc.vector.tensor_copy(bias_k[:, 0, 0:1], own[:, 0:1]).then_inc(s_init, 2)

            def body(t, edge, odd):
                n = t
                if exists(n):
                    dve.wait_ge(s_v, 2 * n + 2)
                    if not isinstance(n, int) or n > 0:
                        dve.wait_ge(s_pv, NW * n)
                    for im in range(2):
                        last = nc.vector.tensor_scalar(
                            v_own[:, 4:8, :, VC * im:VC * im + HD],
                            ps[0:PAIR, 7, :].rearrange("p (w h d) -> p w h d", w=4, h=NH),
                            own[:, im:im + 1], None, ALU.mult)
                    last.then_inc(s_vown_d, 1)
                n = t - 2
                if exists(n):
                    dve.wait_ge(s_proj, n + 1)
                    dve.wait_ge(s_xres, n + 1)
                    if not isinstance(n, int) or n > 0:
                        dve.wait_ge(s_x1b, n)
                    nc.vector.tensor_tensor(x1[:, :, :], tokens_of(4)[0:TP, 0:WS, :], x_res[:, :, :],
                                            ALU.add).then_inc(s_x1, 1)
                    dve.wait_ge(s_x1, n + 1)
                    moments(n, x1, st2, s_st2, mv2, s_ln2)
                n = t + 1
                if exists(n):
                    if not isinstance(n, int) or n > 0:
                        dve.wait_ge(s_mx_dma, 64 * n)
                        dve.wait_ge(s_st_dma, 192 * n)
                    else:
                        dve.wait_ge(s_initp, 1)
                    for j, (own_hi, pad, bank, b) in enumerate((
                            (q_hi_own, q_hi_pad, 6, BQ), (q_hi_own, q_hi_pad, 7, BQ),
                            (k_hi_own, k_hi_pad, 0, BK), (k_hi_own, k_hi_pad, 1, BK))):
                        im = j % 2
                        dve.wait_ge(s_hi, 4 * n + j + 1)
                        f32 = ps[:, bank, 0:BT].rearrange("p (w q) -> p w q", w=NW)
                        hi = own_hi[:, im, :, im, :]
                        for e in range(2):
                            c0, c1 = e * C // 2, (e + 1) * C // 2
                            nc.vector.tensor_copy(pad[c0:c1, im, e, :].rearrange("p (w q) -> p w q", w=NW),
                                                  hi[c0:c1])
                            if j < 2:
                                last = nc.vector.scalar_tensor_tensor(
                                    q_lo_pad[c0:c1, im, e, :].rearrange("p (w q) -> p w q", w=NW),
                                    f32[c0:c1], col[c0:c1, b:b + 1], hi[c0:c1], ALU.add, ALU.subtract)
                        if j >= 2:
                            last = nc.vector.scalar_tensor_tensor(k_lo_own[:, im, :, im, :], f32, col[:, b:b + 1],
                                                                  hi, ALU.add, ALU.subtract)
                        last.then_inc(s_lo, 1)
                n = t + 2
                if exists(n) and not (isinstance(n, int) and n == 0):
                    norm1(n, edge)
                n = t - 2
                if exists(n):
                    dve.wait_ge(s_t2, n + 1)
                    if not isinstance(n, int) or n > 0:
                        dve.wait_ge(s_fc1, 2 * CH * n)
                    nc.vector.tensor_scalar(hT[:, :].rearrange("p (i c) -> p i c", i=WS), tokens_of(0)[:, 0:WS, 0:TP],
                                            col[:, G2:G2 + 1], col[:, B2:B2 + 1], ALU.mult, ALU.add).then_inc(s_hT, 1)
                for w in range(NW):
                    n = t + 1
                    if exists(n):
                        if w == 0 and (not isinstance(n, int) or n > 0):
                            dve.wait_ge(s_maxT, NW * n)
                        dve.wait_ge(s_rows, NW * n + w + 1)
                        nc.vector.tensor_reduce(
                            neg_max[:, w, :].rearrange("p (b h) -> p b h", b=2),
                            ps[0:PAIR, 0:2, 0:HB * WT].rearrange("p b (h k) -> p b h k", k=WT),
                            AX_X, ALU.max, negate=True).then_inc(s_max, 1)
                    n = t - 2
                    if exists(n) and w in (5, 7):
                        p = w // 2 - 2
                        i0, i1 = HALVES[p]
                        if p == 0:
                            dve.wait_ge(s_x1b, n + 1)
                            if not isinstance(n, int) or n > 0:
                                dve.wait_ge(s_stored, loads(n - 1, edge(n) and (not isinstance(n, int) or edge(n - 1))))
                        dve.wait_ge(s_fc2, 2 * n + p + 1)
                        nc.vector.tensor_tensor(y_out[:, i0:i1, :], tokens_of(6)[0:TP, i0:i1, :], x1_b[:, i0:i1, :],
                                                ALU.add).then_inc(s_fin, 1)
                if exists(t):
                    repeat_sums(t, 0)
                n = t + 1
                if exists(n):
                    dve.wait_ge(s_maxT, NW * (n + 1))
                    if not isinstance(n, int) or n > 0:
                        dve.wait_ge(s_neg_dma, 64 * n)
                    nc.vector.tensor_copy(
                        neg_maxT[:, :, :, :],
                        tokens_of(6)[0:NH, 0:NW, 0:PAIR].rearrange("p w (m q) -> p m w q", m=2)).then_inc(s_negT, 1)
                n = t - 1
                if exists(n):
                    dve.wait_ge(s_o_dma, 256 * (n + 1))
                    nc.vector.reciprocal(r_sums[:, :, :], sums[:, :, :]).then_inc(s_rsum, 1)
                    dve.wait_ge(s_rsum, n + 1)
                    if not isinstance(n, int) or n > 0:
                        dve.wait_ge(s_proj, n)
                    dst = oT[:, :, :].rearrange("p i (m c) -> p i m c", m=2)
                    a, r = (v[:, :, :].rearrange("p m (w i j) -> p m w i j", w=NW, i=WS) for v in (oT_raw, r_sums))
                    last_w, kept = NW - 1, WS - SS
                    def div(o, a_, r_):
                        return nc.vector.tensor_tensor(o, a_, r_, ALU.mult)
                    for im in range(2):
                        div(dst[:, :, im, SS:SS + last_w * WS].rearrange("p i (w j) -> p i w j", j=WS),
                            a[:, im, 0:last_w].rearrange("p w i j -> p i w j"),
                            r[:, im, 0:last_w].rearrange("p w i j -> p i w j"))
                    div(dst[:, :, :, W - kept:W], a[:, :, last_w, :, 0:kept].rearrange("p m i j -> p i m j"),
                        r[:, :, last_w, :, 0:kept].rearrange("p m i j -> p i m j"))
                    div(dst[:, :, :, 0:SS], a[:, :, last_w, :, kept:WS].rearrange("p m i j -> p i m j"),
                        r[:, :, last_w, :, kept:WS].rearrange("p m i j -> p i m j")).then_inc(s_oT, 1)
                if exists(t):
                    repeat_sums(t, 1)

            turns(dve, body)

        @block.tensor
        def _(pe):
            mm = nc.tensor.matmul
            pe.wait_ge(s_w, 16 * N_W)
            pe.wait_ge(s_const, 16 * 5)
            pe.wait_ge(s_bt, 3)
            mm(ps[0:TP, 7, 0:C], bv_wide[:, :], w_p[:, :], start=True, stop=True).then_inc(s_bp_mm, 1)
            pe.wait_ge(s_bd2, 16 * 2 * WS)
            for h in range(NH):
                last = nc.tensor.transpose(ps[0:WT, h // HB, (h % HB) * WT:(h % HB + 1) * WT],
                                           bias_f[0:WT, h, :], idn[0:WT, 0:WT])
            last.then_inc(s_bt_mm, 1)
            pe.wait_ge(s_inita, 2)
            pe.wait_ge(s_init, 2)
            pe.wait_ge(s_ones, 32)

            def max_logits(n, w, edge):
                if w == 0:
                    pe.wait_ge(s_mx_dma, 64 * (n + 1))
                    if not isinstance(n, int) or n >= 3:
                        pe.wait_ge(s_hT, n - 2)
                else:
                    pe.wait_ge(s_max, NW * n + w)
                for g in range(NH2):
                    last = mm(ps[0:PAIR, g // 4, (g % 4) * PAIR:(g % 4 + 1) * PAIR].rearrange("p (e k) -> p e k", e=2),
                              mx_q[:, g, w * PAIR:(w + 1) * PAIR],
                              mx_k[edge(n)][:, g, :].rearrange("p (e w k) -> p e w k", e=2, w=NW)[:, :, w, :],
                              start=True, stop=True)
                last.then_inc(s_rows, 1)

            def max_transposed(n, w):
                pe.wait_ge(s_max, NW * n + w + 1)
                if w == 0 and (not isinstance(n, int) or n >= 3):
                    pe.wait_ge(s_fin, 2 * (n - 2))
                nc.tensor.transpose(tokens_of(6)[0:NH, w, 0:PAIR], neg_max[:, w, :],
                                    idn[0:PAIR, 0:PAIR]).then_inc(s_maxT, 1)

            def logits(n, w, edge, par):
                if w == 0:
                    pe.wait_ge(s_st_dma, 192 * (n + 1))
                    pe.wait_ge(s_neg_dma, 64 * (n + 1))
                if w > 0 or not isinstance(n, int) or n > 0:
                    pe.wait_ge(s_exp, NW * n + w)
                if w == 4 and (not isinstance(n, int) or n > 1):
                    pe.wait_ge(s_gelu, 2 * CH * (n - 1))
                kind = 2 * edge(n) + (w == NW - 1)
                for b in range(2):
                    mm(ps[0:PAIR, 2 + b, 0:HB * WT], eye_pair[:, :], bias_t[:, kind, b * HB * WT:(b + 1) * HB * WT],
                       start=True, stop=False)
                    for g in range(4 * b, 4 * b + 4):
                        last = mm(ps[0:PAIR, 2 + b, (g % 4) * PAIR:(g % 4 + 1) * PAIR].rearrange("p (e q) -> p e q", e=2),
                                  st_k[par][:, g, w * PAIR:(w + 1) * PAIR],
                                  st_q[par][:, g, :].rearrange("p (e w q) -> p e w q", e=2, w=NW)[:, :, w, :],
                                  start=False, stop=(g % 4 == 3))
                last.then_inc(s_st, 1)

            def pv(n, w):
                pe.wait_ge(s_exp, NW * n + w + 1)
                if w == 0:
                    pe.wait_ge(s_vown_a, n + 1)
                    pe.wait_ge(s_vown_d, n + 1)
                    if not isinstance(n, int) or n > 1:
                        pe.wait_ge(s_x1, n - 1)
                if w in (4, 5) and (not isinstance(n, int) or n > 1):
                    pe.wait_ge(s_gelu, 2 * CH * (n - 1))
                if w >= 2 or not isinstance(n, int) or n > 0:
                    pe.wait_ge(s_pv_sb, NW * n + w - 1)
                for h in range(NH):
                    g, r = h // NR, h % NR
                    last = mm(ps[32 * r:32 * r + 2 * VC, 4 + w % 2, g * WT:(g + 1) * WT],
                              v_own[:, w, h, :], probs[:, w % 2, h * WT:(h + 1) * WT], start=True, stop=True)
                last.then_inc(s_pv, 1)

            def body(t, edge, odd):
                n = t
                if exists(n):
                    pe.wait_ge(s_negT, n + 1)
                    for w in range(NW):
                        last = mm(ps[0:PAIR, 6 + w // 4, (w % 4) * C:(w % 4 + 1) * C], yT[:, w, :, :].rearrange("p m q -> p (m q)"), w_v[:, :],
                                  start=True, stop=True)
                        if w % 4 == 3:
                            last.then_inc(s_v, 1)
                n = t + 1
                if exists(n):
                    pe.wait_ge(s_z1, n + 1)
                    if not isinstance(n, int) or n > 0:
                        pe.wait_ge(s_max, NW * n)
                    for i in range(WS):
                        last = nc.tensor.transpose(tokens_of(0)[:, i, 0:TP], z1[:, i, :], idn[0:TP, 0:TP])
                    last.then_inc(s_t1, 1)
                n = t - 2
                if exists(n):
                    pe.wait_ge(s_oT, n + 1)
                    if exists(n + 1):
                        pe.wait_ge(s_pv_sb, NW * (n + 2))
                    for i in range(WS):
                        last = mm(tokens_of(4)[0:TP, i, :], oT[:, i, :], w_p[:, :], start=True, stop=True)
                    last.then_inc(s_proj, 1)
                n = t + 1
                if exists(n):
                    pe.wait_ge(s_yT, n + 1)
                    if not isinstance(n, int) or n > 0:
                        pe.wait_ge(s_vown_a, n)
                        pe.wait_ge(s_vown_d, n)
                    for j, (wt, bank) in enumerate(((w_q, 6), (w_q, 7), (w_k, 0), (w_k, 1))):
                        mm(ps[:, bank, 0:BT].rearrange("p (w q) -> p w q", w=NW), wt[:, :], yT[:, :, j % 2, :],
                           start=True, stop=True).then_inc(s_qk, 1)
                n = t
                if exists(n):
                    for w in range(4):
                        logits(n, w, edge, odd(0))
                        if w > 0:
                            pv(n, w - 1)

                def fc1(n, m):
                    c, (i0, i1) = m % CH, HALVES[m // CH]
                    if m == 0 and exists(n + 2):
                        pe.wait_ge(s_exp, NW * (n + 2) + 4)
                    if m == 2 and exists(n + 2):
                        pe.wait_ge(s_pv_sb, NW * (n + 2) + 4)
                    if m >= 4:
                        pe.wait_ge(s_gelu, 2 * CH * n + m - 3)
                    mm(ps[:, 2 + m % 4, 0:(i1 - i0) * TP], w_1[:, c * C:(c + 1) * C], hT[:, i0 * TP:i1 * TP],
                       start=True, stop=True).then_inc(s_fc1, 1)

                def fc2(n, i):
                    p = int(i >= HALVES[1][0])
                    if i == HALVES[p][0]:
                        pe.wait_ge(s_gelu, 2 * CH * n + CH * (p + 1))
                    for c in range(CH):
                        last = mm(tokens_of(6)[0:TP, i, :], hid[:, c, i * TP:(i + 1) * TP], w_2[:, c, :],
                                  start=(c == 0), stop=(c == CH - 1))
                    if i == HALVES[p][1] - 1:
                        last.then_inc(s_fc2, 1)

                n = t - 2
                if exists(n):
                    pe.wait_ge(s_z2, n + 1)
                    if exists(n + 3):
                        pe.wait_ge(s_lo, 4 * (n + 4))
                    for i in range(WS):
                        last = nc.tensor.transpose(tokens_of(0)[:, i, 0:TP], z2[:, i, :], idn[0:TP, 0:TP])
                    last.then_inc(s_t2, 1)
                if exists(t):
                    pv(t, 3)
                if exists(n):
                    pe.wait_ge(s_hT, n + 1)
                tail = [(fc1, m) for m in range(2 * CH)] + [(fc2, i) for i in range(WS)]
                at = 0
                for j, (step, arg) in enumerate(tail):
                    if exists(t - 2):
                        step(t - 2, arg)
                    if exists(t + 1) and j * NW >= at * len(tail) and at < NW:
                        max_logits(t + 1, at, edge)
                        at += 1
                for w in range(4, NW + 1):
                    if exists(t) and w < NW:
                        logits(t, w, edge, odd(0))
                    if exists(t + 1) and w < NW:
                        for k in range(2):
                            max_transposed(t + 1, 2 * (w - 4) + k)
                    if exists(t) and w > 4:
                        pv(t, w - 1)

            turns(pe, body)


def kernel(**inputs):
    from concourse import bacc
    from concourse.bass_utils import run_bass_kernel_spmd

    p = {k.removeprefix("L0_conv_"): np.asarray(v) for k, v in inputs.items()}
    by_place = np.arange(C).reshape(NH2, 2, HD).transpose(1, 2, 0).reshape(-1)
    by_quadrant = np.arange(C).reshape(NG, NR, HD).transpose(1, 2, 0).reshape(-1)
    qw, kw, vw = p["qkv_w"][0:C], p["qkv_w"][C:2 * C], p["qkv_w"][2 * C:3 * C]
    qb, kb, vb = p["qkv_b"][0:C], p["qkv_b"][C:2 * C], p["qkv_b"][2 * C:3 * C]
    i, j = np.divmod(np.arange(WT), WS)
    over = WS - SS
    right = (j[:, None] < over) != (j[None, :] < over)
    below = (i[:, None] < over) != (i[None, :] < over)
    masks = np.zeros((2, WT, 4, WT), np.float32)
    for kind, apart in ((1, right), (2, below), (3, right | below)):
        masks[:, :, kind, :] = np.where(apart, np.float32(-100.0), np.float32(0.0))
    ones4 = np.zeros((2, 2, NH2 * NW, 2, WT), np.float16)
    ones4[0, :, :, 0] = 1
    ones4[1, :, :, 1] = 1
    halves = np.zeros((PAIR, 2), np.float32)
    halves[0:WT, 0] = 1
    halves[WT:PAIR, 1] = 1
    arrays = {
        "x": p["x"],
        "wqT": qw[by_place].T, "wkT": kw[by_place].T, "wvT": vw.T, "wpT": p["proj_w"].T[by_quadrant],
        "w1T": p["fc1_w"].T, "w2T": p["fc2_w"].T,
        "cols": np.stack([p["norm1_g"], p["norm1_b"], p["norm2_g"], p["norm2_b"], qb[by_place], kb[by_place],
                          vb[by_quadrant]] + [p["fc1_b"][c * C:(c + 1) * C] for c in range(CH)], axis=1),
        "rows": np.stack([p["proj_b"], p["fc2_b"]]),
        "tableT": p["rel_pos_table"].T,
        "ident": np.eye(C, dtype=np.float32),
        "eye2": np.tile(np.eye(WT, dtype=np.float16), (2, 2)),
        "wmask": halves, "part": halves,
        "masks": masks.reshape(PAIR, 4, WT),
        "ones4": ones4.reshape(4, NH2, NW * PAIR),
    }
    arrays = {k: np.ascontiguousarray(v) for k, v in arrays.items()}
    nc = bacc.Bacc("TRN2", target_bir_lowering=False, num_devices=1)
    aps = [nc.dram_tensor(f"in_{k}", list(v.shape), mybir.dt.from_np(v.dtype), kind="ExternalInput").ap()
           for k, v in arrays.items()]
    out = nc.dram_tensor("out_y", [B, H, W, C], F32, kind="ExternalOutput").ap()
    swin_block_kernel(nc, *aps, out)
    r = run_bass_kernel_spmd(nc, [{f"in_{k}": v for k, v in arrays.items()}], core_ids=[0])
    return r.results[0]["out_y"]
```

```python
from contextlib import ExitStack

import numpy as np
import concourse.bass as bass
from concourse import mybir

F32 = mybir.dt.float32
F16 = mybir.dt.float16
ALU = mybir.AluOpType
ACT = mybir.ActivationFunctionType
AX_X = mybir.AxisListType.X

B, H, W, C = 32, 56, 56, 128
WS, SS = 7, 3
NH = 16
HD = C // NH
HID = 4 * C
CH = HID // C
NW = W // WS
WT = WS * WS
BT = NW * WT
TP = 2 * W
PAIR = 2 * WT
PAIRS_OF_IMAGES = B // 2
BANDS = H // WS
STEPS = BANDS * PAIRS_OF_IMAGES
EDGE = (BANDS - 1) * PAIRS_OF_IMAGES
HB = NH // 2
VC = HD + 1
NG, NR = 4, 4
EPS = 1e-5
HALVES = ((0, 4), (4, 7))
NH2 = NH // 2
GR = 2 * HD
ST_ROWS = 6 * GR + 4
MX_ROWS = WT + 2 * GR
LOW_SCALE = 2048.0
LOOP_1 = (3, EDGE - 3)
LOOP_2 = (EDGE + 3, STEPS - 3)


def swin_block_kernel(nc, x, wqT, wkT, wvT, wpT, w1T, w2T, cols, rows, tableT, ident, eye2,
                      wmask, part, masks, ones4, spread, out):
    xr = x.rearrange("b h w c -> (b h) w c")
    outr = out.rearrange("b h w c -> (b h) w c")
    ctx = ExitStack()

    def sb(name, shape, dt=F32):
        return ctx.enter_context(nc.sbuf_tensor(name, shape, dt))

    def sem(name):
        return ctx.enter_context(nc.semaphore(name))

    with ctx:
        w_q, w_k, w_v, w_p = (sb(n, [C, C]) for n in ("w_q", "w_k", "w_v", "w_p"))
        w_1 = sb("w_1", [C, HID])
        w_2 = sb("w_2", [C, CH, C])
        col = sb("col", [C, 7 + CH])
        G1, B1, G2, B2, BQ, BK, BV, BF = range(8)
        proj_b = sb("proj_b", [TP, C])
        fc2_b = sb("fc2_b", [TP, C])
        bv_wide = sb("bv_wide", [C, TP])
        idn = sb("idn", [C, C])
        idn16 = sb("idn16", [WT, WT], F16)
        eye_pair = sb("eye_pair", [PAIR, PAIR], F16)
        own = sb("own", [PAIR, 2])
        is_part = sb("is_part", [PAIR, 2])
        mask = sb("mask", [PAIR, 4, WT])
        bias_t = sb("bias_t", [PAIR, 4, NH * WT], F16)
        scrap = sb("scrap", [1, 1])
        half = sb("half", [TP, WS])
        x_in = sb("x_in", [TP, WS, C])
        st1, st2 = sb("st1", [TP, WS, 6]), sb("st2", [TP, WS, 6])
        mv1, mv2 = sb("mv1", [TP, WS, 2]), sb("mv2", [TP, WS, 2])
        ve1, ve2 = sb("ve1", [TP, WS]), sb("ve2", [TP, WS])
        rs1, rs2 = sb("rs1", [TP, WS]), sb("rs2", [TP, WS])
        mr1, mr2 = sb("mr1", [TP, WS]), sb("mr2", [TP, WS])
        nm1, nm2 = sb("nm1", [TP, WS]), sb("nm2", [TP, WS])
        z1, z2 = sb("z1", [TP, WS, C]), sb("z2", [TP, WS, C])
        yT = sb("yT", [C, NW, 2, WT])
        q_hi_own, k_hi_own, k_lo_own = (sb(n, [C, 2, NW, 2, WT], F16)
                                        for n in ("q_hi_own", "k_hi_own", "k_lo_own"))
        q_hi_pad, q_lo_pad, k_hi_pad = (sb(n, [C, 2, 2, BT], F16) for n in ("q_hi_pad", "q_lo_pad", "k_hi_pad"))
        mx_q = sb("mx_q", [MX_ROWS, NH2, NW * PAIR], F16)
        mx_k = [sb(f"mx_k{e}", [MX_ROWS, NH2, 2 * BT], F16) for e in range(2)]
        st_q = [sb(f"st_q{e}", [ST_ROWS, NH2, 2 * BT], F16) for e in range(2)]
        st_k = [sb(f"st_k{e}", [ST_ROWS, NH2, NW * PAIR], F16) for e in range(2)]
        neg_max = sb("neg_max", [PAIR, NW, NH])
        neg_maxT = sb("neg_maxT", [NH, 2, NW, WT], F16)
        v_own = sb("v_own", [PAIR, NW, NH, 2 * VC])
        probs = sb("probs", [PAIR, 2, NH * WT])
        pv_sb = sb("pv_sb", [C, NG, BT])
        oT_raw = sb("oT_raw", [C, 2, BT])
        sums, r_sums, r_rest = (sb(n, [C, 2, WT]) for n in ("sums", "r_sums", "r_rest"))
        r_hi, r_lo = (sb(n, [C, 2, WT], F16) for n in ("r_hi", "r_lo"))
        r_rows = sb("r_rows", [2 * NH, NW, PAIR], F16)
        sel = sb("sel", [2 * NH, C], F16)
        oT = sb("oT", [C, WS, TP])
        x_res = sb("x_res", [TP, WS, C])
        x1 = sb("x1", [TP, WS, C])
        x1_b = sb("x1_b", [TP, WS, C])
        hT = sb("hT", [C, WS * TP])
        hid = sb("hid", [C, CH, WS * TP])
        y_out = sb("y_out", [TP, WS, C])
        bias_f, bias_k = (hid[0:PAIR, j, :].rearrange("p (h q) -> p h q", h=NH) for j in range(2))
        bias_hi, bias_lo = (hid[0:PAIR, 2, :].bitcast(F16).rearrange("p (a h q) -> p a h q", a=2, h=NH)[:, a]
                            for a in range(2))
        bias_r = hid[0:WT, 3, :].rearrange("p (h q) -> p h q", h=NH)
        bias_dram = nc.dram_tensor("bias_dram", [WS, NH, (2 * WS - 1) * WS], F32, kind="Internal").ap()

        ps = ctx.enter_context(nc.psum_tensor("ps", [C, 8, 512], F32))

        s_apart = {nc.gpsimd.engine: sem("waits_of_gpsimd"), nc.vector.engine: sem("waits_of_vector"),
                   nc.sync.engine: sem("waits_of_sync")}

        def tokens_of(bank):
            return ps[:, bank:bank + 2, :].rearrange("p b (i c) -> p (b i) c", c=C)

        (s_w, s_const, s_x, s_st1, s_ln1, s_ve1, s_rs1, s_mr1, s_nm1, s_z1, s_t1, s_yT, s_qk, s_hi, s_lo,
         s_v, s_vown, s_mx_dma, s_rows, s_max, s_maxT, s_negT, s_st_dma, s_neg_dma,
         s_st, s_exp, s_pv, s_pv_sb, s_o_dma, s_sum_dma, s_rsum, s_r_hi, s_r_rest, s_r_lo, s_rr_dma, s_spread, s_oT, s_proj, s_xres_dma, s_xres, s_x1,
         s_st2, s_ln2, s_ve2, s_rs2, s_mr2, s_nm2, s_z2, s_x1b, s_t2, s_hT, s_fc1, s_gelu, s_fc2,
         s_fin, s_stored, s_bd1, s_bd2, s_init, s_initp, s_inita, s_bt, s_bt_mm, s_bp_mm, s_ones) = (
            sem(n) for n in (
                "weights_in", "constants_in", "x_loaded", "stats1_done", "moments1_done", "var_eps1_done",
                "rstd1_done", "mean_rstd1_done", "neg_mean1_done", "z1_ready", "z1_transposed", "yT_ready",
                "qk_projected", "qk_high_ready", "qk_low_ready", "v_projected", "v_own_ready", "max_operands_in", "max_logits_ready", "max_taken", "max_transposed",
                "neg_maxT_ready", "core_operands_in", "neg_max_in", "logits_ready", "exp_done", "pv_done",
                "pv_copied", "o_in", "sums_in", "r_sums_ready", "r_high_ready", "r_rest_ready", "r_low_ready", "r_rows_in",
                "r_spread", "oT_ready", "projected", "x_res_loaded",
                "x_res_biased", "x1_ready", "stats2_done", "moments2_done", "var_eps2_done", "rstd2_done",
                "mean_rstd2_done", "neg_mean2_done", "z2_ready", "x1_biased", "z2_transposed", "hT_ready",
                "fc1_done", "gelu_done", "fc2_done", "y_ready", "y_stored", "bias_strips_out", "bias_in",
                "vector_set_up", "gpsimd_set_up", "scalar_set_up", "bias_step", "bias_transposed",
                "proj_bias_ready", "ones_in"))

        def exists(n):
            return not isinstance(n, int) or 0 <= n < STEPS

        def loads(n, edge):
            return 64 * (n + 1) - 32 * EDGE if edge else 32 * (n + 1)

        def band_dmas(eng, dram, tile, n, edge, store, signal):
            for im in range(2):
                if edge:
                    base = (n - EDGE) * (2 * H) + im * H
                    pieces = ((base + H - WS + SS, 0, WS - SS), (base, WS - SS, SS))
                else:
                    base = (n % PAIRS_OF_IMAGES) * (2 * H) + (n // PAIRS_OF_IMAGES) * WS + SS + im * H
                    pieces = ((base, 0, WS),)
                for row, i0, k in pieces:
                    d = dram[bass.ds(row, k), :, :].rearrange("r w c -> w r c")
                    s = tile[W * im:W * im + W, i0:i0 + k, :]
                    eng.dma_start(d if store else s, s if store else d).then_inc(signal, 16)

        def apart(eng, sem_, value):
            eng.wait_ge(sem_, value)
            eng.sem_inc(s_apart[eng.engine], 1)

        def turns(eng, body):
            def plain(a, b):
                for t in range(a, b):
                    body(t, lambda n: n >= EDGE, lambda k: (t + k) % 2)
            def loop(a, b, edge):
                with eng.Fori(a, b - 1, 2) as t:
                    for later in range(2):
                        body(t + later, lambda n: edge, lambda k: (a + later + k) % 2)
            plain(-2, LOOP_1[0])
            loop(*LOOP_1, False)
            plain(LOOP_1[1], LOOP_2[0])
            loop(*LOOP_2, True)
            plain(LOOP_2[1], STEPS + 2)

        N_W, N_CONST = 9, 6
        block = ctx.enter_context(nc.Block())

        @block.sync
        def _(sp):
            for im, n in ((0, 0),):
                band_dmas(sp, xr, x_in, 0, False, False, s_x)
            for dst, src in ((w_q, wqT), (w_k, wkT), (w_v, wvT), (w_p, wpT), (w_1, w1T), (col, cols)):
                sp.dma_start(dst[:, :], src).then_inc(s_w, 16)
            sp.dma_start(w_2[:, :, :], w2T.rearrange("(a p) n -> p a n", p=C)).then_inc(s_w, 16)
            sp.dma_start(proj_b[:, :], rows[0:1, :].to_broadcast([TP, C])).then_inc(s_w, 16)
            sp.dma_start(fc2_b[:, :], rows[1:2, :].to_broadcast([TP, C])).then_inc(s_w, 16)
            strips = tableT.rearrange("h (a b) -> (h a) b", b=2 * WS - 1)
            for jk in range(WS):
                sp.dma_start(bias_dram[jk].rearrange("h (a b) -> (h a) b", b=WS),
                             strips[:, WS - 1 - jk:2 * WS - 1 - jk]).then_inc(s_bd1, 16)
            sp.wait_ge(s_bd1, 16 * WS)
            for copy in range(2):
                for ik in range(WS):
                    r = copy * WT + ik * WS
                    sp.dma_start(bias_f[r:r + WS, :, :],
                                 bias_dram[:, :, (WS - 1 - ik) * WS:(WS - 1 - ik) * WS + WT]).then_inc(s_bd2, 16)

            def body(t, edge, odd):
                n = t - 1
                if exists(n):
                    apart(sp, s_pv_sb, NW * (n + 1))
                    if not isinstance(n, int) or n > 0:
                        apart(sp, s_rsum, n)
                    for im in range(2):
                        sp.dma_start(sums[:, im, :], pv_sb[VC * im + HD:C:32, :, :]).then_inc(s_sum_dma, 16)
                    if not isinstance(n, int) or n > 0:
                        apart(sp, s_x1, n)
                    band_dmas(sp, xr, x_res, n, edge(n), False, s_xres_dma)
                    if not isinstance(n, int) or n > 0:
                        sp.wait_ge(s_oT, n)
                    for r in range(NR):
                        for im in range(2):
                            p = 32 * r + VC * im
                            sp.dma_start(oT_raw[32 * r:32 * r + 32, im, :],
                                         pv_sb[p:p + HD, :, :]).then_inc(s_o_dma, 16)
                    if not isinstance(n, int) or n > 0:
                        apart(sp, s_spread, n)
                    sp.wait_ge(s_r_lo, n + 1)
                    for k, r_part in enumerate((r_hi, r_lo)):
                        sp.dma_start(r_rows[NH * k:NH * (k + 1), :, :],
                                     r_part[:, :, :].rearrange("p m q -> p (m q)")).then_inc(s_rr_dma, 16)
                n = t + 1
                if exists(n):
                    if not isinstance(n, int) or n > 0:
                        apart(sp, s_rows, NW * n)
                    else:
                        sp.wait_ge(s_init, 2)
                    sp.wait_ge(s_lo, 4 * (n + 1))
                    for im in range(2):
                        rows_ = slice(WT + GR * im, WT + GR * (im + 1))
                        sp.dma_start(mx_k[edge(n)][rows_, :, :],
                                     k_hi_pad[:, im, :, :].rearrange("c e q -> c (e q)")).then_inc(s_mx_dma, 16)
                        sp.dma_start(mx_q[rows_, :, :],
                                     q_hi_own[:, im, :, :, :].rearrange("c w m q -> c (w m q)")
                                     ).then_inc(s_mx_dma, 16)
                    if not isinstance(n, int) or n > 1:
                        sp.wait_ge(s_st, NW * (n - 1))
                    for p, (qq, kk) in enumerate(((q_hi_pad, k_hi_own), (q_hi_pad, k_lo_own),
                                                  (q_lo_pad, k_hi_own))):
                        for im in range(2):
                            rows_ = slice(2 * GR * p + GR * im, 2 * GR * p + GR * (im + 1))
                            sp.dma_start(st_q[odd(1)][rows_, :, :],
                                         qq[:, im, :, :].rearrange("c e q -> c (e q)")).then_inc(s_st_dma, 16)
                            sp.dma_start(st_k[odd(1)][rows_, :, :],
                                         kk[:, im, :, :, :].rearrange("c w m q -> c (w m q)")
                                         ).then_inc(s_st_dma, 16)
                n = t + 3
                if exists(n):
                    sp.wait_ge(s_z1, n)
                    band_dmas(sp, xr, x_in, n, edge(n), False, s_x)
                n = t - 2
                if exists(n):
                    sp.wait_ge(s_fin, 2 * (n + 1))
                    band_dmas(sp, outr, y_out, n, edge(n), True, s_stored)
                n = t + 1
                if exists(n):
                    sp.wait_ge(s_negT, n + 1)
                    for im in range(2):
                        for e in range(2):
                            row = 6 * GR + 2 * im + e
                            sp.dma_start(st_q[odd(1)][row:row + 1, :, e * BT:(e + 1) * BT],
                                         neg_maxT[e:NH:2, im, :, :].rearrange("h w q -> h (w q)")
                                         ).then_inc(s_neg_dma, 16)

            turns(sp, body)
            sp.wait_ge(s_stored, loads(STEPS - 1, True))

        @block.gpsimd
        def _(pool):
            for dst, src in ((idn, ident), (eye_pair, eye2), (own, wmask), (is_part, part), (sel, spread)):
                pool.dma_start(dst[:, :], src).then_inc(s_const, 16)
            pool.dma_start(mask[:, :, :], masks).then_inc(s_const, 16)
            nc.gpsimd.memset(half[:, :], -0.5)
            for tile in (q_hi_own, k_hi_own, k_lo_own):
                nc.gpsimd.memset(tile[:, :, :, :, :], 0.0)
            for tile in (q_hi_pad, q_lo_pad, k_hi_pad):
                last = nc.gpsimd.memset(tile[:, :, :, :], 0.0)
            for e in range(2):
                pool.dma_start(st_k[e][6 * GR:6 * GR + 4, :, :], ones4).then_inc(s_ones, 16)
            last.then_inc(s_initp, 1)

            def norm(n, s_mom, mv, ve, s_ve, rs, s_rs, mr, s_mr, nm, s_nm, src, z, s_free, s_z):
                apart(pool, s_mom, n + 1)
                nc.gpsimd.tensor_scalar(ve[:, :], mv[:, :, 1], 1.0, EPS, ALU.mult, ALU.add).then_inc(s_ve, 1)
                pool.wait_ge(s_ve, n + 1)
                nc.gpsimd.tensor_tensor(rs[:, :], ve[:, :], half[:, :], ALU.pow).then_inc(s_rs, 1)
                pool.wait_ge(s_rs, n + 1)
                nc.gpsimd.tensor_tensor(mr[:, :], mv[:, :, 0], rs[:, :], ALU.mult).then_inc(s_mr, 1)
                apart(pool, s_mr, n + 1)
                nc.gpsimd.tensor_scalar(nm[:, :], mr[:, :], -1.0, 0.0, ALU.mult, ALU.add).then_inc(s_nm, 1)
                pool.wait_ge(s_nm, n + 1)
                if not isinstance(n, int) or n > 0:
                    apart(pool, s_free, n)
                for i in range(WS):
                    last = nc.gpsimd.tensor_scalar(z[:, i, :], src[:, i, :], rs[:, i:i + 1], nm[:, i:i + 1],
                                                   ALU.mult, ALU.add)
                last.then_inc(s_z, 1)

            def body(t, edge, odd):
                n = t - 1
                if exists(n):
                    apart(pool, s_rsum, n + 1)
                    if not isinstance(n, int) or n > 0:
                        apart(pool, s_rr_dma, 32 * n)
                    nc.gpsimd.tensor_scalar(r_hi[:, :, :], r_sums[:, :, :], 1.0, 0.0,
                                            ALU.mult, ALU.add).then_inc(s_r_hi, 1)
                    pool.wait_ge(s_r_hi, n + 1)
                    nc.gpsimd.tensor_tensor(r_rest[:, :, :], r_sums[:, :, :], r_hi[:, :, :],
                                            ALU.subtract).then_inc(s_r_rest, 1)
                    apart(pool, s_r_rest, n + 1)
                    nc.gpsimd.tensor_scalar(r_lo[:, :, :], r_rest[:, :, :], LOW_SCALE, 0.0,
                                            ALU.mult, ALU.add).then_inc(s_r_lo, 1)
                    if isinstance(n, int) and n == 0:
                        pool.wait_ge(s_w, 16 * N_W)
                        pool.wait_ge(s_init, 2)
                    pool.wait_ge(s_xres_dma, loads(n, edge(n)))
                    nc.gpsimd.tensor_tensor(x_res[:, :, :], x_res[:, :, :],
                                            proj_b[:, :].unsqueeze(1).to_broadcast([TP, WS, C]),
                                            ALU.add).then_inc(s_xres, 1)
                n = t + 2
                if exists(n):
                    norm(n, s_ln1, mv1, ve1, s_ve1, rs1, s_rs1, mr1, s_mr1, nm1, s_nm1, x_in, z1, s_t1, s_z1)
                n = t - 1
                if exists(n):
                    norm(n, s_ln2, mv2, ve2, s_ve2, rs2, s_rs2, mr2, s_mr2, nm2, s_nm2, x1, z2, s_t2, s_z2)
                    if not isinstance(n, int) or n > 0:
                        pool.wait_ge(s_fin, 2 * n)
                    nc.gpsimd.tensor_tensor(x1_b[:, :, :], x1[:, :, :],
                                            fc2_b[:, :].unsqueeze(1).to_broadcast([TP, WS, C]),
                                            ALU.add).then_inc(s_x1b, 1)

            turns(pool, body)

        @block.scalar
        def _(act):
            act.wait_ge(s_w, 16 * N_W)
            nc.scalar.mul(w_q[:, :], w_q[:, :], HD ** -0.5).then_inc(s_inita, 1)
            nc.scalar.mul(col[:, BQ:BQ + 1], col[:, BQ:BQ + 1], HD ** -0.5).then_inc(s_inita, 1)
            act.wait_ge(s_inita, 2)

            def load_table(function):
                nc.scalar.activation(scrap[:, :], col[0:1, 0:1], function)

            def exp_pair(n, w):
                act.wait_ge(s_st, NW * n + w + 1)
                if w >= 2 or not isinstance(n, int) or n > 0:
                    act.wait_ge(s_pv, NW * n + w - 1)
                nc.scalar.activation(probs[:, w % 2, :].rearrange("p (b c) -> p b c", b=2),
                                     ps[0:PAIR, 2:4, 0:HB * WT], ACT.Exp).then_inc(s_exp, 1)

            def copy_pv(n, w):
                act.wait_ge(s_pv, NW * n + w + 1)
                if w == 0 and (not isinstance(n, int) or n > 0):
                    act.wait_ge(s_o_dma, 128 * n)
                    act.wait_ge(s_sum_dma, 32 * n)
                nc.scalar.activation(pv_sb[:, :, w * WT:(w + 1) * WT],
                                     ps[:, 4 + w % 2, 0:NG * WT].rearrange("p (g q) -> p g q", g=NG),
                                     ACT.Copy).then_inc(s_pv_sb, 1)

            def gelu(n, m):
                c, (i0, i1) = m % CH, HALVES[m // CH]
                if m == 0 and (not isinstance(n, int) or n > 0):
                    act.wait_ge(s_fc2, 2 * n)
                act.wait_ge(s_fc1, 2 * CH * n + m + 1)
                nc.scalar.activation(hid[:, c, i0 * TP:i1 * TP], ps[:, 2 + m % 4, 0:(i1 - i0) * TP],
                                     ACT.Gelu, bias=col[:, BF + c:BF + c + 1]).then_inc(s_gelu, 1)

            def body(t, edge, odd):
                n = t + 1
                if exists(n):
                    act.wait_ge(s_t1, n + 1)
                    if not isinstance(n, int) or n > 0:
                        act.wait_ge(s_qk, 4 * n)
                        act.wait_ge(s_v, 2 * n)
                    src = tokens_of(0)[:, 0:WS, 0:TP].rearrange("p i (m c) -> p i m c", m=2)
                    dst = yT[:, :, :, :].rearrange("p w m (i j) -> p m w i j", i=WS)
                    last_w = NW - 1
                    kept = WS - SS
                    def put(o, a):
                        return nc.scalar.activation(o, a, ACT.Identity, scale=col[:, G1:G1 + 1],
                                                    bias=col[:, B1:B1 + 1])
                    for im in range(2):
                        put(dst[:, im, 0:last_w, :, :].rearrange("p w i j -> p i w j"),
                            src[:, :, im, SS:SS + last_w * WS].rearrange("p i (w j) -> p i w j", j=WS))
                    put(dst[:, :, last_w, :, 0:kept].rearrange("p m i j -> p i m j"),
                        src[:, :, :, W - kept:W])
                    put(dst[:, :, last_w, :, kept:WS].rearrange("p m i j -> p i m j"),
                        src[:, :, :, 0:SS]).then_inc(s_yT, 1)
                if exists(t - 2):
                    gelu(t - 2, 0)
                if exists(n):
                    if not isinstance(n, int) or n > 0:
                        act.wait_ge(s_mx_dma, 64 * n)
                        act.wait_ge(s_st_dma, 192 * n)
                    else:
                        act.wait_ge(s_initp, 1)
                    for j, (own_hi, bank, b) in enumerate(((q_hi_own, 6, BQ), (q_hi_own, 7, BQ),
                                                           (k_hi_own, 0, BK), (k_hi_own, 1, BK))):
                        im = j % 2
                        act.wait_ge(s_qk, 4 * n + j + 1)
                        nc.scalar.activation(own_hi[:, im, :, im, :],
                                             ps[:, bank, 0:BT].rearrange("p (w q) -> p w q", w=NW), ACT.Identity,
                                             bias=col[:, b:b + 1]).then_inc(s_hi, 1)
                if exists(t - 2):
                    for m in range(1, 2 * CH):
                        gelu(t - 2, m)
                if exists(t):
                    load_table(ACT.Exp)
                    for w in range(NW):
                        exp_pair(t, w)
                        if w > 0:
                            copy_pv(t, w - 1)
                    load_table(ACT.Gelu)
                    copy_pv(t, NW - 1)

            turns(act, body)

        @block.vector
        def _(dve):
            steps = [0]

            def then(ins):
                steps[0] += 1
                ins.then_inc(s_bt, 1)
                dve.wait_ge(s_bt, steps[0])

            def stats(src, st, rows_):
                for i in range(*rows_):
                    last = nc.vector.bn_stats(st[:, i, :], src[:, i, :])
                return last

            def aggregate(n, st, s_st_, mv, s_mv):
                apart(dve, s_st_, n + 1)
                for i in range(WS):
                    last = nc.vector.bn_aggr(mv[:, i, :], st[:, i, :])
                last.then_inc(s_mv, 1)

            def norm1(n, edge):
                dve.wait_ge(s_x, loads(n, edge(n)))
                if not isinstance(n, int) or n > 0:
                    dve.wait_ge(s_z1, n)
                stats(x_in, st1, (0, WS)).then_inc(s_st1, 1)
                aggregate(n, st1, s_st1, mv1, s_ln1)

            norm1(0, lambda n: False)
            nc.vector.memset(ps[:, 4:6, 0:NG * WT], 0.0)
            nc.vector.memset(bv_wide[:, :], 0.0)
            for e in range(2):
                nc.vector.memset(st_q[e][6 * GR:6 * GR + 4, :, :], 0.0)
            then(nc.vector.memset(v_own[:, :, :, :], 0.0))
            dve.wait_ge(s_const, 16 * N_CONST)
            dve.wait_ge(s_w, 16 * N_W)
            then(nc.vector.tensor_copy(idn16[:, :], idn[0:WT, 0:WT]))
            nc.vector.tensor_copy(mx_q[0:WT, :, :].rearrange("p g (w q) -> p (g w) q", q=WT),
                                  idn16[:, :].unsqueeze(1).to_broadcast([WT, NH2 * NW * 2, WT]))
            for im in range(2):
                nc.vector.tensor_copy(v_own[:, :, :, VC * im + HD].rearrange("p w h -> p (w h)"),
                                      own[:, im:im + 1].to_broadcast([PAIR, NW * NH]))
            then(nc.vector.tensor_scalar(bv_wide[:, :], bv_wide[:, :], col[:, BV:BV + 1], None, ALU.add))
            dve.wait_ge(s_bp_mm, 1)
            then(nc.vector.tensor_tensor(proj_b[:, :], proj_b[:, :], ps[0:TP, 7, 0:C], ALU.add))
            dve.wait_ge(s_bd2, 16 * 2 * WS)
            for kind in range(4):
                then(nc.vector.tensor_tensor(bias_k[:, :, :], bias_f[:, :, :],
                                             mask[:, kind, :].unsqueeze(1).to_broadcast([PAIR, NH, WT]), ALU.add))
                then(nc.vector.tensor_copy(bias_hi[:, :, :], bias_k[:, :, :]))
                then(nc.vector.tensor_tensor(bias_lo[:, :, :], bias_k[:, :, :], bias_hi[:, :, :], ALU.subtract))
                then(nc.vector.tensor_scalar(bias_lo[:, :, :], bias_lo[:, :, :], is_part[:, 1:2], None, ALU.mult))
                then(nc.vector.scalar_tensor_tensor(bias_t[:, kind, :], bias_hi[:, :, :].rearrange("p h q -> p (h q)"),
                                                    is_part[:, 0:1],
                                                    bias_lo[:, :, :].rearrange("p h q -> p (h q)"),
                                                    ALU.mult, ALU.add))
            dve.wait_ge(s_bt_mm, 1)
            for b in range(2):
                then(nc.vector.tensor_copy(bias_r[:, HB * b:HB * (b + 1), :],
                                           ps[0:WT, b, 0:HB * WT].rearrange("p (h k) -> p h k", h=HB)))
            for kind in range(4):
                first = kind % 2 == 0
                for w in (range(NW - 1) if first else (NW - 1,)):
                    last = nc.vector.tensor_tensor(
                        mx_k[kind // 2][0:WT, :, :].rearrange("p g (e w k) -> p (g e) w k", e=2, w=NW)[:, :, w, :],
                        bias_r[:, :, :],
                        mask[0:WT, kind, :].unsqueeze(1).to_broadcast([WT, NH, WT]), ALU.add)
            then(last)
            nc.vector.tensor_copy(bias_k[:, 0, 0:1], own[:, 0:1]).then_inc(s_init, 2)

            def finish(n, p, edge):
                i0, i1 = HALVES[p]
                if p == 0:
                    dve.wait_ge(s_x1b, n + 1)
                    if not isinstance(n, int) or n > 0:
                        dve.wait_ge(s_stored, loads(n - 1, edge(n) and (not isinstance(n, int) or edge(n - 1))))
                dve.wait_ge(s_fc2, 2 * n + p + 1)
                nc.vector.tensor_tensor(y_out[:, i0:i1, :], tokens_of(6)[0:TP, i0:i1, :], x1_b[:, i0:i1, :],
                                        ALU.add).then_inc(s_fin, 1)

            def body(t, edge, odd):
                n = t
                if exists(n):
                    if not isinstance(n, int) or n > 0:
                        dve.wait_ge(s_pv, NW * n)
                    for b in range(2):
                        dve.wait_ge(s_v, 2 * n + b + 1)
                        for im in range(2):
                            last = nc.vector.tensor_scalar(
                                v_own[:, 4 * b:4 * b + 4, :, VC * im:VC * im + HD],
                                ps[0:PAIR, 6 + b, :].rearrange("p (w h d) -> p w h d", w=4, h=NH),
                                own[:, im:im + 1], None, ALU.mult)
                        last.then_inc(s_vown, 1)
                n = t - 1
                if exists(n):
                    dve.wait_ge(s_sum_dma, 32 * (n + 1))
                    if not isinstance(n, int) or n > 0:
                        dve.wait_ge(s_r_lo, n)
                    nc.vector.reciprocal(r_sums[:, :, :], sums[:, :, :]).then_inc(s_rsum, 1)
                n = t + 1
                if exists(n):
                    if not isinstance(n, int) or n > 0:
                        dve.wait_ge(s_mx_dma, 64 * n)
                        dve.wait_ge(s_st_dma, 192 * n)
                    else:
                        dve.wait_ge(s_initp, 1)
                    for j, (own_hi, pad, bank, b) in enumerate((
                            (q_hi_own, q_hi_pad, 6, BQ), (q_hi_own, q_hi_pad, 7, BQ),
                            (k_hi_own, k_hi_pad, 0, BK), (k_hi_own, k_hi_pad, 1, BK))):
                        im = j % 2
                        dve.wait_ge(s_hi, 4 * n + j + 1)
                        f32 = ps[:, bank, 0:BT].rearrange("p (w q) -> p w q", w=NW)
                        hi = own_hi[:, im, :, im, :]
                        for e in range(2):
                            c0, c1 = e * C // 2, (e + 1) * C // 2
                            nc.vector.tensor_copy(pad[c0:c1, im, e, :].rearrange("p (w q) -> p w q", w=NW),
                                                  hi[c0:c1])
                            if j < 2:
                                last = nc.vector.scalar_tensor_tensor(
                                    q_lo_pad[c0:c1, im, e, :].rearrange("p (w q) -> p w q", w=NW),
                                    f32[c0:c1], col[c0:c1, b:b + 1], hi[c0:c1], ALU.add, ALU.subtract)
                        if j >= 2:
                            last = nc.vector.scalar_tensor_tensor(k_lo_own[:, im, :, im, :], f32, col[:, b:b + 1],
                                                                  hi, ALU.add, ALU.subtract)
                        last.then_inc(s_lo, 1)
                n = t + 2
                if exists(n) and not (isinstance(n, int) and n == 0):
                    norm1(n, edge)
                if exists(t - 2):
                    finish(t - 2, 0, edge)
                n = t - 1
                if exists(n):
                    dve.wait_ge(s_o_dma, 128 * (n + 1))
                    dve.wait_ge(s_spread, n + 1)
                    if not isinstance(n, int) or n > 0:
                        dve.wait_ge(s_proj, n)
                    dst = oT[:, :, :].rearrange("p i (m c) -> p i m c", m=2)
                    a = oT_raw[:, :, :].rearrange("p m (w i j) -> p m w i j", w=NW, i=WS)
                    r = tokens_of(4)[:, :, 0:PAIR].rearrange("p w (m i j) -> p m w i j", m=2, i=WS)
                    last_w, kept = NW - 1, WS - SS
                    def div(o, a_, r_):
                        return nc.vector.tensor_tensor(o, a_, r_, ALU.mult)
                    for im in range(2):
                        div(dst[:, :, im, SS:SS + last_w * WS].rearrange("p i (w j) -> p i w j", j=WS),
                            a[:, im, 0:last_w].rearrange("p w i j -> p i w j"),
                            r[:, im, 0:last_w].rearrange("p w i j -> p i w j"))
                    div(dst[:, :, :, W - kept:W], a[:, :, last_w, :, 0:kept].rearrange("p m i j -> p i m j"),
                        r[:, :, last_w, :, 0:kept].rearrange("p m i j -> p i m j"))
                    div(dst[:, :, :, 0:SS], a[:, :, last_w, :, kept:WS].rearrange("p m i j -> p i m j"),
                        r[:, :, last_w, :, kept:WS].rearrange("p m i j -> p i m j")).then_inc(s_oT, 1)
                if exists(t - 2):
                    finish(t - 2, 1, edge)
                n = t - 1
                if exists(n):
                    dve.wait_ge(s_proj, n + 1)
                    dve.wait_ge(s_xres, n + 1)
                    if not isinstance(n, int) or n > 0:
                        dve.wait_ge(s_x1b, n)
                    nc.vector.tensor_tensor(x1[:, :, :], tokens_of(4)[0:TP, 0:WS, :], x_res[:, :, :],
                                            ALU.add).then_inc(s_x1, 1)
                    dve.wait_ge(s_x1, n + 1)
                for w in range(NW):
                    n = t + 1
                    if exists(n):
                        dve.wait_ge(s_rows, NW * n + w + 1)
                        if w == 0 and (not isinstance(n, int) or n > 0):
                            dve.wait_ge(s_maxT, NW * n)
                        nc.vector.tensor_reduce(
                            neg_max[:, w, :].rearrange("p (b h) -> p b h", b=2),
                            ps[0:PAIR, 0:2, 0:HB * WT].rearrange("p b (h k) -> p b h k", k=WT),
                            AX_X, ALU.max, negate=True).then_inc(s_max, 1)
                    n = t - 1
                    if exists(n):
                        if w < 2:
                            stats(x1, st2, (2 * w, 2 * w + 2))
                        if w == 2:
                            stats(x1, st2, (4, WS)).then_inc(s_st2, 1)
                        if w == 3:
                            aggregate(n, st2, s_st2, mv2, s_ln2)
                n = t + 1
                if exists(n):
                    dve.wait_ge(s_maxT, NW * (n + 1))
                    if not isinstance(n, int) or n > 0:
                        dve.wait_ge(s_neg_dma, 64 * n)
                    nc.vector.tensor_copy(
                        neg_maxT[:, :, :, :],
                        tokens_of(6)[0:NH, 0:NW, 0:PAIR].rearrange("p w (m q) -> p m w q", m=2)).then_inc(s_negT, 1)
                n = t - 1
                if exists(n):
                    dve.wait_ge(s_t2, n + 1)
                    if not isinstance(n, int) or n > 0:
                        dve.wait_ge(s_fc1, 2 * CH * n)
                    nc.vector.tensor_scalar(hT[:, :].rearrange("p (i c) -> p i c", i=WS), tokens_of(0)[:, 0:WS, 0:TP],
                                            col[:, G2:G2 + 1], col[:, B2:B2 + 1], ALU.mult, ALU.add).then_inc(s_hT, 1)

            turns(dve, body)

        @block.tensor
        def _(pe):
            mm = nc.tensor.matmul
            pe.wait_ge(s_w, 16 * N_W)
            pe.wait_ge(s_const, 16 * N_CONST)
            pe.wait_ge(s_bt, 3)
            mm(ps[0:TP, 7, 0:C], bv_wide[:, :], w_p[:, :], start=True, stop=True).then_inc(s_bp_mm, 1)
            pe.wait_ge(s_bd2, 16 * 2 * WS)
            for h in range(NH):
                last = nc.tensor.transpose(ps[0:WT, h // HB, (h % HB) * WT:(h % HB + 1) * WT],
                                           bias_f[0:WT, h, :], idn[0:WT, 0:WT])
            last.then_inc(s_bt_mm, 1)
            pe.wait_ge(s_inita, 2)
            pe.wait_ge(s_init, 2)
            pe.wait_ge(s_ones, 32)

            def max_logits(n, w, edge):
                if w == 0:
                    pe.wait_ge(s_mx_dma, 64 * (n + 1))
                else:
                    pe.wait_ge(s_max, NW * n + w)
                for g in range(NH2):
                    last = mm(ps[0:PAIR, g // 4, (g % 4) * PAIR:(g % 4 + 1) * PAIR].rearrange("p (e k) -> p e k", e=2),
                              mx_q[:, g, w * PAIR:(w + 1) * PAIR],
                              mx_k[edge(n)][:, g, :].rearrange("p (e w k) -> p e w k", e=2, w=NW)[:, :, w, :],
                              start=True, stop=True)
                last.then_inc(s_rows, 1)

            def max_transposed(n, w):
                pe.wait_ge(s_max, NW * n + w + 1)
                if w == 0 and (not isinstance(n, int) or n >= 3):
                    pe.wait_ge(s_fin, 2 * (n - 2))
                nc.tensor.transpose(tokens_of(6)[0:NH, w, 0:PAIR], neg_max[:, w, :],
                                    idn[0:PAIR, 0:PAIR]).then_inc(s_maxT, 1)

            def logits(n, w, edge, par):
                if w == 0:
                    pe.wait_ge(s_st_dma, 192 * (n + 1))
                    pe.wait_ge(s_neg_dma, 64 * (n + 1))
                    if not isinstance(n, int) or n > 1:
                        pe.wait_ge(s_gelu, 2 * CH * (n - 1))
                if w > 0 or not isinstance(n, int) or n > 0:
                    pe.wait_ge(s_exp, NW * n + w)
                kind = 2 * edge(n) + (w == NW - 1)
                for b in range(2):
                    mm(ps[0:PAIR, 2 + b, 0:HB * WT], eye_pair[:, :], bias_t[:, kind, b * HB * WT:(b + 1) * HB * WT],
                       start=True, stop=False)
                    for g in range(4 * b, 4 * b + 4):
                        last = mm(ps[0:PAIR, 2 + b, (g % 4) * PAIR:(g % 4 + 1) * PAIR].rearrange("p (e q) -> p e q", e=2),
                                  st_k[par][:, g, w * PAIR:(w + 1) * PAIR],
                                  st_q[par][:, g, :].rearrange("p (e w q) -> p e w q", e=2, w=NW)[:, :, w, :],
                                  start=False, stop=(g % 4 == 3))
                last.then_inc(s_st, 1)

            def pv(n, w):
                pe.wait_ge(s_exp, NW * n + w + 1)
                if w == 0:
                    pe.wait_ge(s_vown, 2 * (n + 1))
                    if not isinstance(n, int) or n > 0:
                        pe.wait_ge(s_x1, n)
                if w >= 2 or not isinstance(n, int) or n > 0:
                    pe.wait_ge(s_pv_sb, NW * n + w - 1)
                for h in range(NH):
                    g, r = h // NR, h % NR
                    last = mm(ps[32 * r:32 * r + 2 * VC, 4 + w % 2, g * WT:(g + 1) * WT],
                              v_own[:, w, h, :], probs[:, w % 2, h * WT:(h + 1) * WT], start=True, stop=True)
                last.then_inc(s_pv, 1)

            def fc1(n, m):
                c, (i0, i1) = m % CH, HALVES[m // CH]
                if m == 0:
                    pe.wait_ge(s_hT, n + 1)
                    if exists(n + 1):
                        pe.wait_ge(s_exp, NW * (n + 2))
                if m == 2 and exists(n + 1):
                    pe.wait_ge(s_pv_sb, NW * (n + 2))
                if m >= 4:
                    pe.wait_ge(s_gelu, 2 * CH * n + m - 3)
                mm(ps[:, 2 + m % 4, 0:(i1 - i0) * TP], w_1[:, c * C:(c + 1) * C], hT[:, i0 * TP:i1 * TP],
                   start=True, stop=True).then_inc(s_fc1, 1)

            def fc2(n, p):
                if p == 0:
                    if exists(n + 3):
                        pe.wait_ge(s_lo, 4 * (n + 3) + 2)
                    elif exists(n + 2):
                        pe.wait_ge(s_vown, 2 * (n + 3))
                pe.wait_ge(s_gelu, 2 * CH * n + CH * (p + 1))
                for i in range(*HALVES[p]):
                    for c in range(CH):
                        last = mm(tokens_of(6)[0:TP, i, :], hid[:, c, i * TP:(i + 1) * TP], w_2[:, c, :],
                                  start=(c == 0), stop=(c == CH - 1))
                last.then_inc(s_fc2, 1)

            def body(t, edge, odd):
                n = t
                if exists(n):
                    pe.wait_ge(s_negT, n + 1)
                    for w in range(NW):
                        last = mm(tokens_of(6)[0:PAIR, w, :], yT[:, w, :, :].rearrange("p m q -> p (m q)"), w_v[:, :],
                                  start=True, stop=True)
                        if w % 4 == 3:
                            last.then_inc(s_v, 1)
                n = t + 1
                if exists(n):
                    pe.wait_ge(s_z1, n + 1)
                    if not isinstance(n, int) or n > 2:
                        pe.wait_ge(s_hT, n - 2)
                    for i in range(WS):
                        last = nc.tensor.transpose(tokens_of(0)[:, i, 0:TP], z1[:, i, :], idn[0:TP, 0:TP])
                    last.then_inc(s_t1, 1)
                if exists(t - 2):
                    for m in range(3):
                        fc1(t - 2, m)
                if exists(n):
                    pe.wait_ge(s_yT, n + 1)
                    if not isinstance(n, int) or n > 0:
                        pe.wait_ge(s_vown, 2 * n)
                    for j, (wt, bank) in enumerate(((w_q, 6), (w_q, 7), (w_k, 0), (w_k, 1))):
                        mm(ps[:, bank, 0:BT].rearrange("p (w q) -> p w q", w=NW), wt[:, :], yT[:, :, j % 2, :],
                           start=True, stop=True).then_inc(s_qk, 1)
                n = t - 2
                if exists(n):
                    for m in range(3, 2 * CH):
                        fc1(n, m)
                    fc2(n, 0)
                    pe.wait_ge(s_gelu, 2 * CH * (n + 1))
                if exists(t):
                    logits(t, 0, edge, odd(0))
                n = t - 1
                if exists(n):
                    pe.wait_ge(s_rr_dma, 32 * (n + 1))
                    for b in range(2):
                        last = mm(tokens_of(4)[:, 4 * b:4 * b + 4, 0:PAIR], sel[:, :], r_rows[:, 4 * b:4 * b + 4, :],
                                  start=True, stop=True)
                    last.then_inc(s_spread, 1)
                if exists(t - 2):
                    fc2(t - 2, 1)
                if exists(n):
                    pe.wait_ge(s_oT, n + 1)
                    for i in range(WS):
                        last = mm(tokens_of(4)[0:TP, i, :], oT[:, i, :], w_p[:, :], start=True, stop=True)
                    last.then_inc(s_proj, 1)
                for w in range(NW):
                    if exists(t) and w > 0:
                        logits(t, w, edge, odd(0))
                        pv(t, w - 1)
                    if exists(t + 1):
                        max_logits(t + 1, w, edge)
                        if w > 0:
                            max_transposed(t + 1, w - 1)
                if exists(t):
                    pv(t, NW - 1)
                if exists(t + 1):
                    max_transposed(t + 1, NW - 1)
                n = t - 1
                if exists(n):
                    pe.wait_ge(s_z2, n + 1)
                    for i in range(WS):
                        last = nc.tensor.transpose(tokens_of(0)[:, i, 0:TP], z2[:, i, :], idn[0:TP, 0:TP])
                    last.then_inc(s_t2, 1)

            turns(pe, body)


def kernel(**inputs):
    from concourse import bacc
    from concourse.bass_utils import run_bass_kernel_spmd

    p = {k.removeprefix("L0_conv_"): np.asarray(v) for k, v in inputs.items()}
    by_place = np.arange(C).reshape(NH2, 2, HD).transpose(1, 2, 0).reshape(-1)
    by_quadrant = np.arange(C).reshape(NG, NR, HD).transpose(1, 2, 0).reshape(-1)
    qw, kw, vw = p["qkv_w"][0:C], p["qkv_w"][C:2 * C], p["qkv_w"][2 * C:3 * C]
    qb, kb, vb = p["qkv_b"][0:C], p["qkv_b"][C:2 * C], p["qkv_b"][2 * C:3 * C]
    i, j = np.divmod(np.arange(WT), WS)
    over = WS - SS
    right = (j[:, None] < over) != (j[None, :] < over)
    below = (i[:, None] < over) != (i[None, :] < over)
    masks = np.zeros((2, WT, 4, WT), np.float32)
    for kind, apart in ((1, right), (2, below), (3, right | below)):
        masks[:, :, kind, :] = np.where(apart, np.float32(-100.0), np.float32(0.0))
    ones4 = np.zeros((2, 2, NH2 * NW, 2, WT), np.float16)
    ones4[0, :, :, 0] = 1
    ones4[1, :, :, 1] = 1
    spread = np.zeros((2, NR, NG, NR, HD, NG), np.float16)
    for r in range(NR):
        for g in range(NG):
            spread[0, r, g, r, :, g] = 1
            spread[1, r, g, r, :, g] = 1 / LOW_SCALE
    halves = np.zeros((PAIR, 2), np.float32)
    halves[0:WT, 0] = 1
    halves[WT:PAIR, 1] = 1
    arrays = {
        "x": p["x"],
        "wqT": qw[by_place].T, "wkT": kw[by_place].T, "wvT": vw.T, "wpT": p["proj_w"].T[by_quadrant],
        "w1T": p["fc1_w"].T, "w2T": p["fc2_w"].T,
        "cols": np.stack([p["norm1_g"], p["norm1_b"], p["norm2_g"], p["norm2_b"], qb[by_place], kb[by_place],
                          vb[by_quadrant]] + [p["fc1_b"][c * C:(c + 1) * C] for c in range(CH)], axis=1),
        "rows": np.stack([p["proj_b"], p["fc2_b"]]),
        "tableT": p["rel_pos_table"].T,
        "ident": np.eye(C, dtype=np.float32),
        "eye2": np.tile(np.eye(WT, dtype=np.float16), (2, 2)),
        "wmask": halves, "part": halves,
        "masks": masks.reshape(PAIR, 4, WT),
        "ones4": ones4.reshape(4, NH2, NW * PAIR),
        "spread": spread.reshape(2 * NH, C),
    }
    arrays = {k: np.ascontiguousarray(v) for k, v in arrays.items()}
    nc = bacc.Bacc("TRN2", target_bir_lowering=False, num_devices=1)
    aps = [nc.dram_tensor(f"in_{k}", list(v.shape), mybir.dt.from_np(v.dtype), kind="ExternalInput").ap()
           for k, v in arrays.items()]
    out = nc.dram_tensor("out_y", [B, H, W, C], F32, kind="ExternalOutput").ap()
    swin_block_kernel(nc, *aps, out)
    r = run_bass_kernel_spmd(nc, [{f"in_{k}": v for k, v in arrays.items()}], core_ids=[0])
    return r.results[0]["out_y"]
```

```python
from contextlib import ExitStack

import numpy as np
import concourse.bass as bass
from concourse import mybir

F32 = mybir.dt.float32
F16 = mybir.dt.float16
ALU = mybir.AluOpType
ACT = mybir.ActivationFunctionType
AX_X = mybir.AxisListType.X

B, H, W, C = 32, 56, 56, 128
WS, SS = 7, 3
NH = 16
HD = C // NH
HID = 4 * C
CH = HID // C
NW = W // WS
WT = WS * WS
BT = NW * WT
TP = 2 * W
PAIR = 2 * WT
PAIRS_OF_IMAGES = B // 2
BANDS = H // WS
STEPS = BANDS * PAIRS_OF_IMAGES
EDGE = (BANDS - 1) * PAIRS_OF_IMAGES
HB = NH // 2
VC = HD + 1
NG, NR = 4, 4
EPS = 1e-5
HALVES = ((0, 4), (4, 7))
NH2 = NH // 2
GR = 2 * HD
ST_ROWS = 6 * GR + 4
MX_ROWS = WT + 2 * GR
W_SCALE = 64.0
LOW_SCALE = 2048.0
LOOP_1 = (3, EDGE - 3)
LOOP_2 = (EDGE + 3, STEPS - 3)


def swin_block_kernel(nc, x, wqT, wkT, wvT, wpT, w1T, w2T, cols, rows, tableT, ident, eye2,
                      wmask, part, masks, ones4, spread, out):
    xr = x.rearrange("b h w c -> (b h) w c")
    outr = out.rearrange("b h w c -> (b h) w c")
    ctx = ExitStack()

    def sb(name, shape, dt=F32):
        return ctx.enter_context(nc.sbuf_tensor(name, shape, dt))

    def sem(name):
        return ctx.enter_context(nc.semaphore(name))

    with ctx:
        w_q, w_k, w_v, w_p = (sb(n, [C, C]) for n in ("w_q", "w_k", "w_v", "w_p"))
        w_1 = sb("w_1", [C, HID])
        w1_hi, w1_lo = (sb(n, [C, HID], F16) for n in ("w1_hi", "w1_lo"))
        w_2 = sb("w_2", [C, CH, C])
        col = sb("col", [C, 7 + CH])
        G1, B1, G2, B2, BQ, BK, BV, BF = range(8)
        proj_b = sb("proj_b", [TP, C])
        fc2_b = sb("fc2_b", [TP, C])
        bv_wide = sb("bv_wide", [C, TP])
        idn = sb("idn", [C, C])
        idn16 = sb("idn16", [WT, WT], F16)
        eye_pair = sb("eye_pair", [PAIR, PAIR], F16)
        own = sb("own", [PAIR, 2])
        is_part = sb("is_part", [PAIR, 2])
        mask = sb("mask", [PAIR, 4, WT])
        bias_t = sb("bias_t", [PAIR, 4, NH * WT], F16)
        scrap = sb("scrap", [1, 1])
        half = sb("half", [TP, WS])
        x_in = sb("x_in", [TP, WS, C])
        st1, st2 = sb("st1", [TP, WS, 6]), sb("st2", [TP, WS, 6])
        mv1, mv2 = sb("mv1", [TP, WS, 2]), sb("mv2", [TP, WS, 2])
        ve1, ve2 = sb("ve1", [TP, WS]), sb("ve2", [TP, WS])
        rs1, rs2 = sb("rs1", [TP, WS]), sb("rs2", [TP, WS])
        mr1, mr2 = sb("mr1", [TP, WS]), sb("mr2", [TP, WS])
        nm1, nm2 = sb("nm1", [TP, WS]), sb("nm2", [TP, WS])
        z1, z2 = sb("z1", [TP, WS, C]), sb("z2", [TP, WS, C])
        yT = [sb(f"yT{e}", [C, NW, 2, WT]) for e in range(2)]
        q_hi_own, k_hi_own, k_lo_own = (sb(n, [C, 2, NW, 2, WT], F16)
                                        for n in ("q_hi_own", "k_hi_own", "k_lo_own"))
        q_hi_pad, q_lo_pad, k_hi_pad = (sb(n, [C, 2, 2, BT], F16) for n in ("q_hi_pad", "q_lo_pad", "k_hi_pad"))
        mx_q = sb("mx_q", [MX_ROWS, NH2, NW * PAIR], F16)
        mx_k = [sb(f"mx_k{e}", [MX_ROWS, NH2, 2 * BT], F16) for e in range(2)]
        st_q = [sb(f"st_q{e}", [ST_ROWS, NH2, 2 * BT], F16) for e in range(2)]
        st_k = [sb(f"st_k{e}", [ST_ROWS, NH2, NW * PAIR], F16) for e in range(2)]
        neg_max = sb("neg_max", [PAIR, NW, NH])
        neg_maxT = sb("neg_maxT", [NH, 2, NW, WT], F16)
        v_own = sb("v_own", [PAIR, NW, NH, 2 * VC])
        probs = sb("probs", [PAIR, 2, NH * WT])
        pv_sb = sb("pv_sb", [C, NG, BT])
        oT_raw = sb("oT_raw", [C, 2, BT])
        sums, r_sums, r_rest = (sb(n, [C, 2, WT]) for n in ("sums", "r_sums", "r_rest"))
        r_hi, r_lo = (sb(n, [C, 2, WT], F16) for n in ("r_hi", "r_lo"))
        r_rows = sb("r_rows", [2 * NH, NW, PAIR], F16)
        sel = sb("sel", [2 * NH, C], F16)
        oT = sb("oT", [C, WS, TP])
        x_res = sb("x_res", [TP, WS, C])
        x1 = sb("x1", [TP, WS, C])
        x1_b = sb("x1_b", [TP, WS, C])
        h_hi, h_lo = (sb(n, [C, WS * TP], F16) for n in ("h_hi", "h_lo"))
        hid = sb("hid", [C, CH, WS * TP])
        y_out = sb("y_out", [TP, WS, C])
        bias_f, bias_k = (hid[0:PAIR, j, :].rearrange("p (h q) -> p h q", h=NH) for j in range(2))
        bias_hi, bias_lo = (hid[0:PAIR, 2, :].bitcast(F16).rearrange("p (a h q) -> p a h q", a=2, h=NH)[:, a]
                            for a in range(2))
        bias_r = hid[0:WT, 3, :].rearrange("p (h q) -> p h q", h=NH)
        bias_dram = nc.dram_tensor("bias_dram", [WS, NH, (2 * WS - 1) * WS], F32, kind="Internal").ap()

        ps = ctx.enter_context(nc.psum_tensor("ps", [C, 8, 512], F32))

        s_apart = {nc.gpsimd.engine: sem("waits_of_gpsimd"), nc.vector.engine: sem("waits_of_vector"),
                   nc.sync.engine: sem("waits_of_sync")}

        def tokens_of(bank):
            return ps[:, bank:bank + 2, :].rearrange("p b (i c) -> p (b i) c", c=C)

        (s_w, s_const, s_x, s_st1, s_ln1, s_ve1, s_rs1, s_mr1, s_nm1, s_z1, s_t1, s_yT, s_qk, s_hi, s_lo,
         s_v, s_vown, s_mx_dma, s_rows, s_max, s_maxT, s_negT, s_st_dma, s_neg_dma, s_st, s_exp, s_pv,
         s_pv_sb, s_o_dma, s_sum_dma, s_rsum, s_r_hi, s_r_rest, s_r_lo, s_rr_dma, s_spread, s_oT, s_proj,
         s_xres_dma, s_xres, s_x1, s_st2, s_ln2, s_ve2, s_rs2, s_mr2, s_nm2, s_z2, s_x1b, s_t2, s_h_hi,
         s_h_lo, s_fc1, s_gelu, s_fc2, s_fin, s_stored, s_bd1, s_bd2, s_init, s_initp, s_inita, s_bt,
         s_bt_mm, s_bp_mm, s_ones) = (
            sem(n) for n in (
                "weights_in", "constants_in", "x_loaded", "stats1_done", "moments1_done", "var_eps1_done",
                "rstd1_done", "mean_rstd1_done", "neg_mean1_done", "z1_ready", "z1_transposed", "yT_ready",
                "qk_projected", "qk_high_ready", "qk_low_ready", "v_projected", "v_own_ready",
                "max_operands_in", "max_logits_ready", "max_taken", "max_transposed", "neg_maxT_ready",
                "core_operands_in", "neg_max_in", "logits_ready", "exp_done", "pv_done", "pv_copied",
                "o_in", "sums_in", "r_sums_ready", "r_high_ready", "r_rest_ready", "r_low_ready",
                "r_rows_in", "r_spread", "oT_ready", "projected", "x_res_loaded", "x_res_biased",
                "x1_ready", "stats2_done", "moments2_done", "var_eps2_done", "rstd2_done",
                "mean_rstd2_done", "neg_mean2_done", "z2_ready", "x1_biased", "z2_transposed",
                "h_high_ready", "h_low_ready", "fc1_done", "gelu_done", "fc2_done", "y_ready", "y_stored",
                "bias_strips_out", "bias_in", "vector_set_up", "gpsimd_set_up", "scalar_set_up",
                "bias_step", "bias_transposed", "proj_bias_ready", "ones_in"))

        def exists(n):
            return not isinstance(n, int) or 0 <= n < STEPS

        def loads(n, edge):
            return 64 * (n + 1) - 32 * EDGE if edge else 32 * (n + 1)

        def band_dmas(eng, dram, tile, n, edge, store, signal):
            for im in range(2):
                if edge:
                    base = (n - EDGE) * (2 * H) + im * H
                    pieces = ((base + H - WS + SS, 0, WS - SS), (base, WS - SS, SS))
                else:
                    base = (n % PAIRS_OF_IMAGES) * (2 * H) + (n // PAIRS_OF_IMAGES) * WS + SS + im * H
                    pieces = ((base, 0, WS),)
                for row, i0, k in pieces:
                    d = dram[bass.ds(row, k), :, :].rearrange("r w c -> w r c")
                    s = tile[W * im:W * im + W, i0:i0 + k, :]
                    eng.dma_start(d if store else s, s if store else d).then_inc(signal, 16)

        def apart(eng, sem_, value):
            eng.wait_ge(sem_, value)
            eng.sem_inc(s_apart[eng.engine], 1)

        def turns(eng, body):
            def plain(a, b):
                for t in range(a, b):
                    body(t, lambda n: n >= EDGE, lambda k: (t + k) % 2)
            def loop(a, b, edge):
                with eng.Fori(a, b - 1, 2) as t:
                    for later in range(2):
                        body(t + later, lambda n: edge, lambda k: (a + later + k) % 2)
            plain(-2, LOOP_1[0])
            loop(*LOOP_1, False)
            plain(LOOP_1[1], LOOP_2[0])
            loop(*LOOP_2, True)
            plain(LOOP_2[1], STEPS + 2)

        N_W, N_CONST = 9, 6
        block = ctx.enter_context(nc.Block())

        @block.sync
        def _(sp):
            band_dmas(sp, xr, x_in, 0, False, False, s_x)
            for dst, src in ((w_q, wqT), (w_k, wkT), (w_v, wvT), (w_p, wpT), (w_1, w1T), (col, cols)):
                sp.dma_start(dst[:, :], src).then_inc(s_w, 16)
            sp.dma_start(w_2[:, :, :], w2T.rearrange("(a p) n -> p a n", p=C)).then_inc(s_w, 16)
            sp.dma_start(proj_b[:, :], rows[0:1, :].to_broadcast([TP, C])).then_inc(s_w, 16)
            sp.dma_start(fc2_b[:, :], rows[1:2, :].to_broadcast([TP, C])).then_inc(s_w, 16)
            strips = tableT.rearrange("h (a b) -> (h a) b", b=2 * WS - 1)
            for jk in range(WS):
                sp.dma_start(bias_dram[jk].rearrange("h (a b) -> (h a) b", b=WS),
                             strips[:, WS - 1 - jk:2 * WS - 1 - jk]).then_inc(s_bd1, 16)
            sp.wait_ge(s_bd1, 16 * WS)
            for copy in range(2):
                for ik in range(WS):
                    r = copy * WT + ik * WS
                    sp.dma_start(bias_f[r:r + WS, :, :],
                                 bias_dram[:, :, (WS - 1 - ik) * WS:(WS - 1 - ik) * WS + WT]).then_inc(s_bd2, 16)

            def body(t, edge, odd):
                n = t - 1
                if exists(n):
                    if not isinstance(n, int) or n > 0:
                        sp.wait_ge(s_oT, n)
                    for r in range(NR):
                        for im in range(2):
                            p = 32 * r + VC * im
                            sp.dma_start(oT_raw[32 * r:32 * r + 32, im, :],
                                         pv_sb[p:p + HD, :, :]).then_inc(s_o_dma, 16)
                    if not isinstance(n, int) or n > 0:
                        apart(sp, s_spread, n)
                    sp.wait_ge(s_r_lo, n + 1)
                    for k, r_part in enumerate((r_hi, r_lo)):
                        sp.dma_start(r_rows[NH * k:NH * (k + 1), :, :],
                                     r_part[:, :, :].rearrange("p m q -> p (m q)")).then_inc(s_rr_dma, 16)
                n = t + 1
                if exists(n):
                    if not isinstance(n, int) or n > 0:
                        apart(sp, s_rows, NW * n)
                    else:
                        sp.wait_ge(s_init, 2)
                    sp.wait_ge(s_lo, 4 * (n + 1))
                    for im in range(2):
                        rows_ = slice(WT + GR * im, WT + GR * (im + 1))
                        sp.dma_start(mx_k[edge(n)][rows_, :, :],
                                     k_hi_pad[:, im, :, :].rearrange("c e q -> c (e q)")).then_inc(s_mx_dma, 16)
                        sp.dma_start(mx_q[rows_, :, :],
                                     q_hi_own[:, im, :, :, :].rearrange("c w m q -> c (w m q)")
                                     ).then_inc(s_mx_dma, 16)
                    if not isinstance(n, int) or n > 1:
                        sp.wait_ge(s_st, 2 * NW * (n - 1))
                    for p, (qq, kk) in enumerate(((q_hi_pad, k_hi_own), (q_hi_pad, k_lo_own),
                                                  (q_lo_pad, k_hi_own))):
                        for im in range(2):
                            rows_ = slice(2 * GR * p + GR * im, 2 * GR * p + GR * (im + 1))
                            sp.dma_start(st_q[odd(1)][rows_, :, :],
                                         qq[:, im, :, :].rearrange("c e q -> c (e q)")).then_inc(s_st_dma, 16)
                            sp.dma_start(st_k[odd(1)][rows_, :, :],
                                         kk[:, im, :, :, :].rearrange("c w m q -> c (w m q)")
                                         ).then_inc(s_st_dma, 16)
                n = t + 3
                if exists(n):
                    sp.wait_ge(s_z1, n)
                    band_dmas(sp, xr, x_in, n, edge(n), False, s_x)
                n = t - 2
                if exists(n):
                    sp.wait_ge(s_fin, 2 * (n + 1))
                    band_dmas(sp, outr, y_out, n, edge(n), True, s_stored)
                n = t
                if exists(n):
                    if not isinstance(n, int) or n > 0:
                        apart(sp, s_x1, 2 * n)
                    band_dmas(sp, xr, x_res, n, edge(n), False, s_xres_dma)
                    if not isinstance(n, int) or n > 0:
                        apart(sp, s_rsum, n)
                    sp.wait_ge(s_pv_sb, NW * (n + 1))
                    for im in range(2):
                        sp.dma_start(sums[:, im, :], pv_sb[VC * im + HD:C:32, :, :]).then_inc(s_sum_dma, 16)
                n = t + 1
                if exists(n):
                    sp.wait_ge(s_negT, n + 1)
                    for im in range(2):
                        for e in range(2):
                            row = 6 * GR + 2 * im + e
                            sp.dma_start(st_q[odd(1)][row:row + 1, :, e * BT:(e + 1) * BT],
                                         neg_maxT[e:NH:2, im, :, :].rearrange("h w q -> h (w q)")
                                         ).then_inc(s_neg_dma, 16)

            turns(sp, body)
            sp.wait_ge(s_stored, loads(STEPS - 1, True))

        @block.gpsimd
        def _(pool):
            for dst, src in ((idn, ident), (eye_pair, eye2), (own, wmask), (is_part, part), (sel, spread)):
                pool.dma_start(dst[:, :], src).then_inc(s_const, 16)
            pool.dma_start(mask[:, :, :], masks).then_inc(s_const, 16)
            nc.gpsimd.memset(half[:, :], -0.5)
            for tile in (q_hi_own, k_hi_own, k_lo_own):
                nc.gpsimd.memset(tile[:, :, :, :, :], 0.0)
            for tile in (q_hi_pad, q_lo_pad, k_hi_pad):
                last = nc.gpsimd.memset(tile[:, :, :, :], 0.0)
            for e in range(2):
                pool.dma_start(st_k[e][6 * GR:6 * GR + 4, :, :], ones4).then_inc(s_ones, 16)
            last.then_inc(s_initp, 1)

            def norm(n, s_mom, mv, ve, s_ve, rs, s_rs, mr, s_mr, nm, s_nm, src, z, s_free, s_z):
                apart(pool, s_mom, n + 1)
                nc.gpsimd.tensor_scalar(ve[:, :], mv[:, :, 1], 1.0, EPS, ALU.mult, ALU.add).then_inc(s_ve, 1)
                pool.wait_ge(s_ve, n + 1)
                nc.gpsimd.tensor_tensor(rs[:, :], ve[:, :], half[:, :], ALU.pow).then_inc(s_rs, 1)
                pool.wait_ge(s_rs, n + 1)
                nc.gpsimd.tensor_tensor(mr[:, :], mv[:, :, 0], rs[:, :], ALU.mult).then_inc(s_mr, 1)
                apart(pool, s_mr, n + 1)
                nc.gpsimd.tensor_scalar(nm[:, :], mr[:, :], -1.0, 0.0, ALU.mult, ALU.add).then_inc(s_nm, 1)
                pool.wait_ge(s_nm, n + 1)
                if not isinstance(n, int) or n > 0:
                    apart(pool, s_free, n)
                for i in range(WS):
                    last = nc.gpsimd.tensor_scalar(z[:, i, :], src[:, i, :], rs[:, i:i + 1], nm[:, i:i + 1],
                                                   ALU.mult, ALU.add)
                last.then_inc(s_z, 1)

            def body(t, edge, odd):
                n = t - 1
                if exists(n):
                    apart(pool, s_rsum, n + 1)
                    if not isinstance(n, int) or n > 0:
                        apart(pool, s_rr_dma, 32 * n)
                    nc.gpsimd.tensor_scalar(r_hi[:, :, :], r_sums[:, :, :], 1.0, 0.0,
                                            ALU.mult, ALU.add).then_inc(s_r_hi, 1)
                    pool.wait_ge(s_r_hi, n + 1)
                    nc.gpsimd.tensor_tensor(r_rest[:, :, :], r_sums[:, :, :], r_hi[:, :, :],
                                            ALU.subtract).then_inc(s_r_rest, 1)
                    apart(pool, s_r_rest, n + 1)
                    nc.gpsimd.tensor_scalar(r_lo[:, :, :], r_rest[:, :, :], LOW_SCALE, 0.0,
                                            ALU.mult, ALU.add).then_inc(s_r_lo, 1)
                    if isinstance(n, int) and n == 0:
                        pool.wait_ge(s_w, 16 * N_W)
                        pool.wait_ge(s_init, 2)
                    pool.wait_ge(s_xres_dma, loads(n, edge(n)))
                    nc.gpsimd.tensor_tensor(x_res[:, :, :], x_res[:, :, :],
                                            proj_b[:, :].unsqueeze(1).to_broadcast([TP, WS, C]),
                                            ALU.add).then_inc(s_xres, 1)
                n = t + 2
                if exists(n):
                    norm(n, s_ln1, mv1, ve1, s_ve1, rs1, s_rs1, mr1, s_mr1, nm1, s_nm1, x_in, z1, s_t1, s_z1)
                n = t - 1
                if exists(n):
                    norm(n, s_ln2, mv2, ve2, s_ve2, rs2, s_rs2, mr2, s_mr2, nm2, s_nm2, x1, z2, s_t2, s_z2)
                    if not isinstance(n, int) or n > 0:
                        pool.wait_ge(s_fin, 2 * n)
                    nc.gpsimd.tensor_tensor(x1_b[:, :, :], x1[:, :, :],
                                            fc2_b[:, :].unsqueeze(1).to_broadcast([TP, WS, C]),
                                            ALU.add).then_inc(s_x1b, 1)

            turns(pool, body)

        @block.scalar
        def _(act):
            act.wait_ge(s_w, 16 * N_W)
            nc.scalar.mul(w_q[:, :], w_q[:, :], HD ** -0.5).then_inc(s_inita, 1)
            nc.scalar.mul(col[:, BQ:BQ + 1], col[:, BQ:BQ + 1], HD ** -0.5).then_inc(s_inita, 1)
            act.wait_ge(s_inita, 2)

            def load_table(function):
                nc.scalar.activation(scrap[:, :], col[0:1, 0:1], function)

            def exp_pair(n, w):
                if w >= 2 or not isinstance(n, int) or n > 0:
                    act.wait_ge(s_pv, NW * n + w - 1)
                for b in range(2):
                    act.wait_ge(s_st, 2 * (NW * n + w) + b + 1)
                    nc.scalar.activation(probs[:, w % 2, b * HB * WT:(b + 1) * HB * WT],
                                         ps[0:PAIR, 2 + b, 0:HB * WT], ACT.Exp).then_inc(s_exp, 1)

            def copy_pv(n, w):
                act.wait_ge(s_pv, NW * n + w + 1)
                if w == 0 and (not isinstance(n, int) or n > 0):
                    act.wait_ge(s_o_dma, 128 * n)
                    act.wait_ge(s_sum_dma, 32 * n)
                nc.scalar.activation(pv_sb[:, :, w * WT:(w + 1) * WT],
                                     ps[:, 4 + w % 2, 0:NG * WT].rearrange("p (g q) -> p g q", g=NG),
                                     ACT.Copy).then_inc(s_pv_sb, 1)

            def gelu(n, m):
                c, (i0, i1) = m % CH, HALVES[m // CH]
                if m == 0 and (not isinstance(n, int) or n > 0):
                    act.wait_ge(s_fc2, 2 * n)
                act.wait_ge(s_fc1, 2 * CH * n + m + 1)
                nc.scalar.activation(hid[:, c, i0 * TP:i1 * TP], ps[:, 2 + m % 4, 0:(i1 - i0) * TP],
                                     ACT.Gelu, bias=col[:, BF + c:BF + c + 1], scale=1 / W_SCALE).then_inc(s_gelu, 1)

            def body(t, edge, odd):
                n = t + 1
                if exists(n):
                    act.wait_ge(s_t1, n + 1)
                    if not isinstance(n, int) or n > 1:
                        act.wait_ge(s_v, 2 * (n - 1))
                    src = tokens_of(0)[:, 0:WS, 0:TP].rearrange("p i (m c) -> p i m c", m=2)
                    dst = yT[odd(1)][:, :, :, :].rearrange("p w m (i j) -> p m w i j", i=WS)
                    last_w = NW - 1
                    kept = WS - SS
                    def put(o, a):
                        return nc.scalar.activation(o, a, ACT.Identity, scale=col[:, G1:G1 + 1],
                                                    bias=col[:, B1:B1 + 1])
                    for im in range(2):
                        put(dst[:, im, 0:last_w, :, :].rearrange("p w i j -> p i w j"),
                            src[:, :, im, SS:SS + last_w * WS].rearrange("p i (w j) -> p i w j", j=WS))
                    put(dst[:, :, last_w, :, 0:kept].rearrange("p m i j -> p i m j"),
                        src[:, :, :, W - kept:W])
                    put(dst[:, :, last_w, :, kept:WS].rearrange("p m i j -> p i m j"),
                        src[:, :, :, 0:SS]).then_inc(s_yT, 1)
                n = t - 2
                if exists(n):
                    act.wait_ge(s_t2, n + 1)
                    if not isinstance(n, int) or n > 0:
                        act.wait_ge(s_fc1, 2 * CH * n)
                    for i0, i1 in HALVES:
                        nc.scalar.activation(h_hi[:, i0 * TP:i1 * TP].rearrange("p (i c) -> p i c", c=TP),
                                             tokens_of(2)[:, i0:i1, 0:TP], ACT.Copy).then_inc(s_h_hi, 1)
                    load_table(ACT.Gelu)
                n = t + 1
                for j, (own_hi, bank, b) in enumerate(((k_hi_own, 0, BK), (k_hi_own, 1, BK),
                                                       (q_hi_own, 6, BQ), (q_hi_own, 7, BQ))):
                    if exists(n):
                        if j == 0:
                            if not isinstance(n, int) or n > 0:
                                act.wait_ge(s_mx_dma, 64 * n)
                                act.wait_ge(s_st_dma, 192 * n)
                            else:
                                act.wait_ge(s_initp, 1)
                        im = j % 2
                        act.wait_ge(s_qk, 4 * n + j + 1)
                        nc.scalar.activation(own_hi[:, im, :, im, :],
                                             ps[:, bank, 0:BT].rearrange("p (w q) -> p w q", w=NW), ACT.Identity,
                                             bias=col[:, b:b + 1]).then_inc(s_hi, 1)
                    if exists(t - 2) and j == 1:
                        gelu(t - 2, 0)
                        gelu(t - 2, 1)
                if exists(t - 2):
                    for m in range(2, 2 * CH):
                        gelu(t - 2, m)
                if exists(t):
                    load_table(ACT.Exp)
                    for w in range(NW):
                        exp_pair(t, w)
                        if w > 0:
                            copy_pv(t, w - 1)
                    copy_pv(t, NW - 1)

            turns(act, body)

        @block.vector
        def _(dve):
            steps = [0]

            def then(ins):
                steps[0] += 1
                ins.then_inc(s_bt, 1)
                dve.wait_ge(s_bt, steps[0])

            def stats(src, st, rows_):
                for i in range(*rows_):
                    last = nc.vector.bn_stats(st[:, i, :], src[:, i, :])
                return last

            def aggregate(n, st, s_st_, mv, s_mv):
                apart(dve, s_st_, n + 1)
                for i in range(WS):
                    last = nc.vector.bn_aggr(mv[:, i, :], st[:, i, :])
                last.then_inc(s_mv, 1)

            def norm1(n, edge):
                dve.wait_ge(s_x, loads(n, edge(n)))
                if not isinstance(n, int) or n > 0:
                    dve.wait_ge(s_z1, n)
                stats(x_in, st1, (0, WS)).then_inc(s_st1, 1)
                aggregate(n, st1, s_st1, mv1, s_ln1)

            norm1(0, lambda n: False)
            nc.vector.memset(ps[:, 4:6, 0:NG * WT], 0.0)
            nc.vector.memset(bv_wide[:, :], 0.0)
            for e in range(2):
                nc.vector.memset(st_q[e][6 * GR:6 * GR + 4, :, :], 0.0)
            then(nc.vector.memset(v_own[:, :, :, :], 0.0))
            dve.wait_ge(s_const, 16 * N_CONST)
            dve.wait_ge(s_w, 16 * N_W)
            then(nc.vector.tensor_copy(idn16[:, :], idn[0:WT, 0:WT]))
            nc.vector.tensor_copy(mx_q[0:WT, :, :].rearrange("p g (w q) -> p (g w) q", q=WT),
                                  idn16[:, :].unsqueeze(1).to_broadcast([WT, NH2 * NW * 2, WT]))
            for im in range(2):
                nc.vector.tensor_copy(v_own[:, :, :, VC * im + HD].rearrange("p w h -> p (w h)"),
                                      own[:, im:im + 1].to_broadcast([PAIR, NW * NH]))
            then(nc.vector.tensor_scalar(bv_wide[:, :], bv_wide[:, :], col[:, BV:BV + 1], None, ALU.add))
            dve.wait_ge(s_bp_mm, 1)
            then(nc.vector.tensor_tensor(col[:, BF:BF + CH], col[:, BF:BF + CH], ps[:, 7, 2 * C:2 * C + CH], ALU.add))
            then(nc.vector.tensor_scalar(w_1[:, :], w_1[:, :], col[:, G2:G2 + 1], W_SCALE, ALU.mult, ALU.mult))
            then(nc.vector.tensor_copy(w1_hi[:, :], w_1[:, :]))
            then(nc.vector.tensor_tensor(w1_lo[:, :], w_1[:, :], w1_hi[:, :], ALU.subtract))
            then(nc.vector.tensor_tensor(proj_b[:, :], proj_b[:, :], ps[0:TP, 7, 0:C], ALU.add))
            dve.wait_ge(s_bd2, 16 * 2 * WS)
            for kind in range(4):
                then(nc.vector.tensor_tensor(bias_k[:, :, :], bias_f[:, :, :],
                                             mask[:, kind, :].unsqueeze(1).to_broadcast([PAIR, NH, WT]), ALU.add))
                then(nc.vector.tensor_copy(bias_hi[:, :, :], bias_k[:, :, :]))
                then(nc.vector.tensor_tensor(bias_lo[:, :, :], bias_k[:, :, :], bias_hi[:, :, :], ALU.subtract))
                then(nc.vector.tensor_scalar(bias_lo[:, :, :], bias_lo[:, :, :], is_part[:, 1:2], None, ALU.mult))
                then(nc.vector.scalar_tensor_tensor(bias_t[:, kind, :], bias_hi[:, :, :].rearrange("p h q -> p (h q)"),
                                                    is_part[:, 0:1],
                                                    bias_lo[:, :, :].rearrange("p h q -> p (h q)"),
                                                    ALU.mult, ALU.add))
            dve.wait_ge(s_bt_mm, 1)
            for b in range(2):
                then(nc.vector.tensor_copy(bias_r[:, HB * b:HB * (b + 1), :],
                                           ps[0:WT, b, 0:HB * WT].rearrange("p (h k) -> p h k", h=HB)))
            for kind in range(4):
                first = kind % 2 == 0
                for w in (range(NW - 1) if first else (NW - 1,)):
                    last = nc.vector.tensor_tensor(
                        mx_k[kind // 2][0:WT, :, :].rearrange("p g (e w k) -> p (g e) w k", e=2, w=NW)[:, :, w, :],
                        bias_r[:, :, :],
                        mask[0:WT, kind, :].unsqueeze(1).to_broadcast([WT, NH, WT]), ALU.add)
            then(last)
            nc.vector.tensor_copy(bias_k[:, 0, 0:1], own[:, 0:1]).then_inc(s_init, 2)

            def finish(n, p, edge):
                i0, i1 = HALVES[p]
                if p == 0:
                    dve.wait_ge(s_x1b, n + 1)
                    if not isinstance(n, int) or n > 0:
                        dve.wait_ge(s_stored, loads(n - 1, edge(n) and (not isinstance(n, int) or edge(n - 1))))
                dve.wait_ge(s_fc2, 2 * n + p + 1)
                nc.vector.tensor_tensor(y_out[:, i0:i1, :], tokens_of(6)[0:TP, i0:i1, :], x1_b[:, i0:i1, :],
                                        ALU.add).then_inc(s_fin, 1)

            def row_maxima(n, w):
                dve.wait_ge(s_rows, NW * n + w + 1)
                if w == 0 and (not isinstance(n, int) or n > 0):
                    dve.wait_ge(s_maxT, NW * n)
                nc.vector.tensor_reduce(
                    neg_max[:, w, :].rearrange("p (b h) -> p b h", b=2),
                    ps[0:PAIR, 0:2, 0:HB * WT].rearrange("p b (h k) -> p b h k", k=WT),
                    AX_X, ALU.max, negate=True).then_inc(s_max, 1)

            def body(t, edge, odd):
                for b in range(2):
                    n = t
                    if exists(n):
                        if b == 0 and (not isinstance(n, int) or n > 0):
                            dve.wait_ge(s_pv, NW * n)
                        dve.wait_ge(s_v, 2 * n + b + 1)
                        for im in range(2):
                            last = nc.vector.tensor_scalar(
                                v_own[:, 4 * b:4 * b + 4, :, VC * im:VC * im + HD],
                                ps[0:PAIR, 6 + b, :].rearrange("p (w h d) -> p w h d", w=4, h=NH),
                                own[:, im:im + 1], None, ALU.mult)
                        last.then_inc(s_vown, 1)
                    n = t - 2
                    if exists(n) and b == 0:
                        for p, (i0, i1) in enumerate(HALVES):
                            dve.wait_ge(s_h_hi, 2 * n + p + 1)
                            high, low = (v[:, i0 * TP:i1 * TP].rearrange("p (i c) -> p i c", c=TP)
                                         for v in (h_hi, h_lo))
                            nc.vector.tensor_tensor(low, tokens_of(2)[:, i0:i1, 0:TP], high,
                                                    ALU.subtract).then_inc(s_h_lo, 1)
                for j, (own_hi, pad, bank, b) in enumerate((
                        (k_hi_own, k_hi_pad, 0, BK), (k_hi_own, k_hi_pad, 1, BK),
                        (q_hi_own, q_hi_pad, 6, BQ), (q_hi_own, q_hi_pad, 7, BQ))):
                    n = t + 1
                    if exists(n):
                        if j == 0:
                            if not isinstance(n, int) or n > 0:
                                dve.wait_ge(s_mx_dma, 64 * n)
                                dve.wait_ge(s_st_dma, 192 * n)
                            else:
                                dve.wait_ge(s_initp, 1)
                        im = j % 2
                        dve.wait_ge(s_hi, 4 * n + j + 1)
                        f32 = ps[:, bank, 0:BT].rearrange("p (w q) -> p w q", w=NW)
                        hi = own_hi[:, im, :, im, :]
                        for e in range(2):
                            c0, c1 = e * C // 2, (e + 1) * C // 2
                            nc.vector.tensor_copy(pad[c0:c1, im, e, :].rearrange("p (w q) -> p w q", w=NW),
                                                  hi[c0:c1])
                            if j >= 2:
                                last = nc.vector.scalar_tensor_tensor(
                                    q_lo_pad[c0:c1, im, e, :].rearrange("p (w q) -> p w q", w=NW),
                                    f32[c0:c1], col[c0:c1, b:b + 1], hi[c0:c1], ALU.add, ALU.subtract)
                        if j < 2:
                            last = nc.vector.scalar_tensor_tensor(k_lo_own[:, im, :, im, :], f32, col[:, b:b + 1],
                                                                  hi, ALU.add, ALU.subtract)
                        last.then_inc(s_lo, 1)
                    n = t - 1
                    if exists(n) and j == 1:
                        dve.wait_ge(s_sum_dma, 32 * (n + 1))
                        if not isinstance(n, int) or n > 0:
                            dve.wait_ge(s_r_lo, n)
                        nc.vector.reciprocal(r_sums[:, :, :], sums[:, :, :]).then_inc(s_rsum, 1)
                n = t + 2
                if exists(n) and not (isinstance(n, int) and n == 0):
                    norm1(n, edge)
                if exists(t - 2):
                    finish(t - 2, 0, edge)
                n = t - 1
                if exists(n):
                    dve.wait_ge(s_o_dma, 128 * (n + 1))
                    dve.wait_ge(s_spread, n + 1)
                    if not isinstance(n, int) or n > 0:
                        dve.wait_ge(s_proj, 2 * n)
                    dst = oT[:, :, :].rearrange("p i (m c) -> p i m c", m=2)
                    a = oT_raw[:, :, :].rearrange("p m (w i j) -> p m w i j", w=NW, i=WS)
                    r = tokens_of(4)[:, :, 0:PAIR].rearrange("p w (m i j) -> p m w i j", m=2, i=WS)
                    last_w, kept = NW - 1, WS - SS
                    def div(o, a_, r_):
                        return nc.vector.tensor_tensor(o, a_, r_, ALU.mult)
                    for im in range(2):
                        div(dst[:, :, im, SS:SS + last_w * WS].rearrange("p i (w j) -> p i w j", j=WS),
                            a[:, im, 0:last_w].rearrange("p w i j -> p i w j"),
                            r[:, im, 0:last_w].rearrange("p w i j -> p i w j"))
                    div(dst[:, :, :, W - kept:W], a[:, :, last_w, :, 0:kept].rearrange("p m i j -> p i m j"),
                        r[:, :, last_w, :, 0:kept].rearrange("p m i j -> p i m j"))
                    div(dst[:, :, :, 0:SS], a[:, :, last_w, :, kept:WS].rearrange("p m i j -> p i m j"),
                        r[:, :, last_w, :, kept:WS].rearrange("p m i j -> p i m j")).then_inc(s_oT, 1)
                if exists(t - 2):
                    finish(t - 2, 1, edge)
                if exists(t + 1):
                    row_maxima(t + 1, 0)
                n = t - 1
                if exists(n):
                    dve.wait_ge(s_xres, n + 1)
                    if not isinstance(n, int) or n > 0:
                        dve.wait_ge(s_x1b, n)
                    for p, (i0, i1) in enumerate(HALVES):
                        dve.wait_ge(s_proj, 2 * n + p + 1)
                        nc.vector.tensor_tensor(x1[:, i0:i1, :], tokens_of(4)[0:TP, i0:i1, :], x_res[:, i0:i1, :],
                                                ALU.add).then_inc(s_x1, 1)
                    dve.wait_ge(s_x1, 2 * (n + 1))
                for w in range(NW):
                    if exists(t + 1) and w > 0:
                        row_maxima(t + 1, w)
                    n = t - 1
                    if exists(n):
                        if w in (1, 2):
                            stats(x1, st2, (2 * w - 2, 2 * w))
                        if w == 3:
                            stats(x1, st2, (4, WS)).then_inc(s_st2, 1)
                        if w == 4:
                            aggregate(n, st2, s_st2, mv2, s_ln2)
                n = t + 1
                if exists(n):
                    dve.wait_ge(s_maxT, NW * (n + 1))
                    if not isinstance(n, int) or n > 0:
                        dve.wait_ge(s_neg_dma, 64 * n)
                    nc.vector.tensor_copy(
                        neg_maxT[:, :, :, :],
                        tokens_of(6)[0:NH, 0:NW, 0:PAIR].rearrange("p w (m q) -> p m w q", m=2)).then_inc(s_negT, 1)
            turns(dve, body)

        @block.tensor
        def _(pe):
            mm = nc.tensor.matmul
            pe.wait_ge(s_w, 16 * N_W)
            pe.wait_ge(s_const, 16 * N_CONST)
            for c in range(CH):
                mm(ps[:, 7, 2 * C + c:2 * C + c + 1], w_1[:, c * C:(c + 1) * C], col[:, B2:B2 + 1],
                   start=True, stop=True)
            pe.wait_ge(s_bt, 3)
            mm(ps[0:TP, 7, 0:C], bv_wide[:, :], w_p[:, :], start=True, stop=True).then_inc(s_bp_mm, 1)
            pe.wait_ge(s_bd2, 16 * 2 * WS)
            for h in range(NH):
                last = nc.tensor.transpose(ps[0:WT, h // HB, (h % HB) * WT:(h % HB + 1) * WT],
                                           bias_f[0:WT, h, :], idn[0:WT, 0:WT])
            last.then_inc(s_bt_mm, 1)
            pe.wait_ge(s_inita, 2)
            pe.wait_ge(s_init, 2)
            pe.wait_ge(s_ones, 32)

            def max_logits(n, w, edge):
                if w == 0:
                    pe.wait_ge(s_mx_dma, 64 * (n + 1))
                else:
                    pe.wait_ge(s_max, NW * n + w)
                for g in range(NH2):
                    last = mm(ps[0:PAIR, g // 4, (g % 4) * PAIR:(g % 4 + 1) * PAIR].rearrange("p (e k) -> p e k", e=2),
                              mx_q[:, g, w * PAIR:(w + 1) * PAIR],
                              mx_k[edge(n)][:, g, :].rearrange("p (e w k) -> p e w k", e=2, w=NW)[:, :, w, :],
                              start=True, stop=True)
                last.then_inc(s_rows, 1)

            def max_transposed(n, w):
                pe.wait_ge(s_max, NW * n + w + 1)
                if w == 0 and (not isinstance(n, int) or n >= 3):
                    pe.wait_ge(s_fin, 2 * (n - 2))
                nc.tensor.transpose(tokens_of(6)[0:NH, w, 0:PAIR], neg_max[:, w, :],
                                    idn[0:PAIR, 0:PAIR]).then_inc(s_maxT, 1)

            def logits(n, w, edge, par):
                if w == 0:
                    pe.wait_ge(s_st_dma, 192 * (n + 1))
                    pe.wait_ge(s_neg_dma, 64 * (n + 1))
                    if not isinstance(n, int) or n > 1:
                        pe.wait_ge(s_gelu, 2 * CH * (n - 1))
                kind = 2 * edge(n) + (w == NW - 1)
                for b in range(2):
                    if w > 0 or not isinstance(n, int) or n > 0:
                        pe.wait_ge(s_exp, 2 * (NW * n + w) + b - 1)
                    mm(ps[0:PAIR, 2 + b, 0:HB * WT], eye_pair[:, :], bias_t[:, kind, b * HB * WT:(b + 1) * HB * WT],
                       start=True, stop=False)
                    for g in range(4 * b, 4 * b + 4):
                        last = mm(ps[0:PAIR, 2 + b, (g % 4) * PAIR:(g % 4 + 1) * PAIR].rearrange("p (e q) -> p e q", e=2),
                                  st_k[par][:, g, w * PAIR:(w + 1) * PAIR],
                                  st_q[par][:, g, :].rearrange("p (e w q) -> p e w q", e=2, w=NW)[:, :, w, :],
                                  start=False, stop=(g % 4 == 3))
                    last.then_inc(s_st, 1)

            def pv(n, w):
                pe.wait_ge(s_exp, 2 * (NW * n + w + 1))
                if w == 0:
                    pe.wait_ge(s_vown, 2 * (n + 1))
                if w < 2 and (not isinstance(n, int) or n > 0):
                    pe.wait_ge(s_x1, 2 * n - 1 + w)
                if w >= 2 or not isinstance(n, int) or n > 0:
                    pe.wait_ge(s_pv_sb, NW * n + w - 1)
                for h in range(NH):
                    g, r = h // NR, h % NR
                    last = mm(ps[32 * r:32 * r + 2 * VC, 4 + w % 2, g * WT:(g + 1) * WT],
                              v_own[:, w, h, :], probs[:, w % 2, h * WT:(h + 1) * WT], start=True, stop=True)
                last.then_inc(s_pv, 1)

            def fc1(n, m):
                c, (i0, i1) = m % CH, HALVES[m // CH]
                if m < 2:
                    pe.wait_ge(s_h_lo, 2 * n + m + 1)
                if m == 0 and exists(n + 1):
                    pe.wait_ge(s_exp, 2 * NW * (n + 2))
                if m == 2 and exists(n + 1):
                    pe.wait_ge(s_pv_sb, NW * (n + 2))
                if m >= 4:
                    pe.wait_ge(s_gelu, 2 * CH * n + m - 3)
                for k, (ww, hh) in enumerate(((w1_hi, h_hi), (w1_hi, h_lo), (w1_lo, h_hi))):
                    last = mm(ps[:, 2 + m % 4, 0:(i1 - i0) * TP], ww[:, c * C:(c + 1) * C], hh[:, i0 * TP:i1 * TP],
                              start=(k == 0), stop=(k == 2))
                last.then_inc(s_fc1, 1)

            def fc2(n, p):
                if exists(n + 3):
                    pe.wait_ge(s_lo, 4 * (n + 3) + 3 + p)
                elif exists(n + 2):
                    pe.wait_ge(s_vown, 2 * (n + 2) + 1 + p)
                pe.wait_ge(s_gelu, 2 * CH * n + CH * (p + 1))
                for i in range(*HALVES[p]):
                    for c in range(CH):
                        last = mm(tokens_of(6)[0:TP, i, :], hid[:, c, i * TP:(i + 1) * TP], w_2[:, c, :],
                                  start=(c == 0), stop=(c == CH - 1))
                last.then_inc(s_fc2, 1)

            def body(t, edge, odd):
                n = t + 1
                if exists(n):
                    pe.wait_ge(s_z1, n + 1)
                    if not isinstance(n, int) or n > 0:
                        pe.wait_ge(s_max, NW * n)
                    for i in range(WS):
                        last = nc.tensor.transpose(tokens_of(0)[:, i, 0:TP], z1[:, i, :], idn[0:TP, 0:TP])
                    last.then_inc(s_t1, 1)
                n = t - 2
                if exists(n):
                    pe.wait_ge(s_z2, n + 1)
                    for i in range(WS):
                        last = nc.tensor.transpose(tokens_of(2)[:, i, 0:TP], z2[:, i, :], idn[0:TP, 0:TP])
                    last.then_inc(s_t2, 1)
                n = t
                if exists(n):
                    pe.wait_ge(s_negT, n + 1)
                    for w in range(NW):
                        last = mm(tokens_of(6)[0:PAIR, w, :], yT[odd(0)][:, w, :, :].rearrange("p m q -> p (m q)"), w_v[:, :],
                                  start=True, stop=True)
                        if w % 4 == 3:
                            last.then_inc(s_v, 1)
                def project(n, j):
                    wt, bank = ((w_k, 0), (w_k, 1), (w_q, 6), (w_q, 7))[j]
                    if j == 0:
                        pe.wait_ge(s_yT, n + 1)
                    if j >= 2 and (not isinstance(n, int) or n > 0):
                        pe.wait_ge(s_vown, 2 * n + j - 3)
                    mm(ps[:, bank, 0:BT].rearrange("p (w q) -> p w q", w=NW), wt[:, :], yT[odd(1)][:, :, j % 2, :],
                       start=True, stop=True).then_inc(s_qk, 1)
                for j in range(2):
                    if exists(t + 1):
                        project(t + 1, j)
                if exists(t - 2):
                    for m in range(2):
                        fc1(t - 2, m)
                for j in range(2, 4):
                    if exists(t + 1):
                        project(t + 1, j)
                n = t - 2
                if exists(n):
                    for m in range(2, 2 * CH):
                        fc1(n, m)
                    fc2(n, 0)
                    pe.wait_ge(s_gelu, 2 * CH * (n + 1))
                if exists(t):
                    logits(t, 0, edge, odd(0))
                n = t - 1
                if exists(n):
                    pe.wait_ge(s_rr_dma, 32 * (n + 1))
                    for b in range(2):
                        last = mm(tokens_of(4)[:, 4 * b:4 * b + 4, 0:PAIR], sel[:, :], r_rows[:, 4 * b:4 * b + 4, :],
                                  start=True, stop=True)
                    last.then_inc(s_spread, 1)
                if exists(t - 2):
                    fc2(t - 2, 1)
                if exists(t + 1):
                    max_logits(t + 1, 0, edge)
                if exists(n):
                    pe.wait_ge(s_oT, n + 1)
                    for i0, i1 in HALVES:
                        for i in range(i0, i1):
                            last = mm(tokens_of(4)[0:TP, i, :], oT[:, i, :], w_p[:, :], start=True, stop=True)
                        last.then_inc(s_proj, 1)
                for w in range(NW):
                    if exists(t + 1) and w > 0:
                        max_logits(t + 1, w, edge)
                    if exists(t) and w > 0:
                        logits(t, w, edge, odd(0))
                        pv(t, w - 1)
                    if exists(t + 1) and w > 0:
                        max_transposed(t + 1, w - 1)
                if exists(t + 1):
                    max_transposed(t + 1, NW - 1)
                if exists(t):
                    pv(t, NW - 1)

            turns(pe, body)


def kernel(**inputs):
    from concourse import bacc
    from concourse.bass_utils import run_bass_kernel_spmd

    p = {k.removeprefix("L0_conv_"): np.asarray(v) for k, v in inputs.items()}
    by_place = np.arange(C).reshape(NH2, 2, HD).transpose(1, 2, 0).reshape(-1)
    by_quadrant = np.arange(C).reshape(NG, NR, HD).transpose(1, 2, 0).reshape(-1)
    qw, kw, vw = p["qkv_w"][0:C], p["qkv_w"][C:2 * C], p["qkv_w"][2 * C:3 * C]
    qb, kb, vb = p["qkv_b"][0:C], p["qkv_b"][C:2 * C], p["qkv_b"][2 * C:3 * C]
    i, j = np.divmod(np.arange(WT), WS)
    over = WS - SS
    right = (j[:, None] < over) != (j[None, :] < over)
    below = (i[:, None] < over) != (i[None, :] < over)
    masks = np.zeros((2, WT, 4, WT), np.float32)
    for kind, apart in ((1, right), (2, below), (3, right | below)):
        masks[:, :, kind, :] = np.where(apart, np.float32(-100.0), np.float32(0.0))
    ones4 = np.zeros((2, 2, NH2 * NW, 2, WT), np.float16)
    ones4[0, :, :, 0] = 1
    ones4[1, :, :, 1] = 1
    spread = np.zeros((2, NR, NG, NR, HD, NG), np.float16)
    for r in range(NR):
        for g in range(NG):
            spread[0, r, g, r, :, g] = 1
            spread[1, r, g, r, :, g] = 1 / LOW_SCALE
    halves = np.zeros((PAIR, 2), np.float32)
    halves[0:WT, 0] = 1
    halves[WT:PAIR, 1] = 1
    arrays = {
        "x": p["x"],
        "wqT": qw[by_place].T, "wkT": kw[by_place].T, "wvT": vw.T, "wpT": p["proj_w"].T[by_quadrant],
        "w1T": p["fc1_w"].T, "w2T": p["fc2_w"].T,
        "cols": np.stack([p["norm1_g"], p["norm1_b"], p["norm2_g"], p["norm2_b"], qb[by_place], kb[by_place],
                          vb[by_quadrant]] + [p["fc1_b"][c * C:(c + 1) * C] for c in range(CH)], axis=1),
        "rows": np.stack([p["proj_b"], p["fc2_b"]]),
        "tableT": p["rel_pos_table"].T,
        "ident": np.eye(C, dtype=np.float32),
        "eye2": np.tile(np.eye(WT, dtype=np.float16), (2, 2)),
        "wmask": halves, "part": halves,
        "masks": masks.reshape(PAIR, 4, WT),
        "ones4": ones4.reshape(4, NH2, NW * PAIR),
        "spread": spread.reshape(2 * NH, C),
    }
    arrays = {k: np.ascontiguousarray(v) for k, v in arrays.items()}
    nc = bacc.Bacc("TRN2", target_bir_lowering=False, num_devices=1)
    aps = [nc.dram_tensor(f"in_{k}", list(v.shape), mybir.dt.from_np(v.dtype), kind="ExternalInput").ap()
           for k, v in arrays.items()]
    out = nc.dram_tensor("out_y", [B, H, W, C], F32, kind="ExternalOutput").ap()
    swin_block_kernel(nc, *aps, out)
    r = run_bass_kernel_spmd(nc, [{f"in_{k}": v for k, v in arrays.items()}], core_ids=[0])
    return r.results[0]["out_y"]
```
